# Optimizing a Trainium2 kernel written in Bass

```python
import numpy as np
import jax
import jax.numpy as jnp

def _softmax(x, axis=-1):
    return jax.nn.softmax(x, axis=axis)

def _gelu(x):
    return jax.nn.gelu(x, approximate=True)

def _silu(x):
    return jax.nn.silu(x)

def _sigmoid(x):
    return jax.nn.sigmoid(x)

def _layernorm(x, axis=-1, eps=1e-05):
    m = jnp.mean(x, axis=axis, keepdims=True)
    v = jnp.var(x, axis=axis, keepdims=True)
    return (x - m) / jnp.sqrt(v + eps)

def _scatter_add(tgt, idx, src, axis=0):
    return tgt.at[idx].add(src)

def _segment_sum(src, seg, n):
    return jax.ops.segment_sum(src, seg, n)
kernel_name = 'mk_seq_preln_d1_jaxref_r8_6383b8'

def setup_inputs(seed: int=0):
    np.random.seed(seed)
    _w = jnp.asarray

    def _L0_attn_setup():
        import jax, jax.numpy as jnp
        import numpy as np
        B, S, H, NH = (2, 256, 128, 16)
        HD = H // NH
        EPS = 1e-06

        def _layernorm(x, scale, bias):
            x32 = x.astype(jnp.float32)
            mean = jnp.mean(x32, axis=-1, keepdims=True)
            var = jnp.mean(jnp.square(x32 - mean), axis=-1, keepdims=True)
            return (x32 - mean) * jax.lax.rsqrt(var + EPS) * scale + bias
        key = jax.random.key(seed)
        ks = jax.random.split(key, 16)
        init = lambda k, shape, fan_in: jax.random.normal(k, shape, jnp.float32) / np.sqrt(fan_in)
        return {'x': jax.random.normal(ks[0], (B, S, H), jnp.float32), 'Wq': init(ks[1], (H, H), H), 'bq': jnp.zeros((H,), jnp.float32), 'Wk': init(ks[2], (H, H), H), 'bk': jnp.zeros((H,), jnp.float32), 'Wv': init(ks[3], (H, H), H), 'bv': jnp.zeros((H,), jnp.float32), 'q_scale': jnp.ones((HD,), jnp.float32), 'q_bias': jnp.zeros((HD,), jnp.float32), 'k_scale': jnp.ones((HD,), jnp.float32), 'k_bias': jnp.zeros((HD,), jnp.float32), 'v_scale': jnp.ones((HD,), jnp.float32), 'v_bias': jnp.zeros((HD,), jnp.float32), 'Wo': init(ks[4], (H, H), H), 'bo': jnp.zeros((H,), jnp.float32)}
    _L0_attn_in = _L0_attn_setup()

    def _L0_ffn_setup():
        import jax, jax.numpy as jnp
        import numpy as np
        DIM = 128
        HIDDEN = 384
        SCALE = 1.0 / 127.0

        def _dequant(w_int, dtype):
            return w_int.astype(dtype) * jnp.asarray(SCALE, dtype)
        key = jax.random.key(seed)
        k_x, k_g, k_u, k_d = jax.random.split(key, 4)
        x = jax.random.normal(k_x, (4, 256, DIM), dtype=jnp.float32)
        w_gate = jax.random.randint(k_g, (HIDDEN, DIM), -127, 128, dtype=jnp.int32)
        w_up = jax.random.randint(k_u, (HIDDEN, DIM), -127, 128, dtype=jnp.int32)
        w_down = jax.random.randint(k_d, (DIM, HIDDEN), -127, 128, dtype=jnp.int32)
        return {'x': x, 'w_gate': w_gate, 'w_up': w_up, 'w_down': w_down}
    _L0_ffn_in = _L0_ffn_setup()
    _d = {'L0_attn_x': _L0_attn_in['x'], 'L0_attn_Wq': _L0_attn_in['Wq'], 'L0_attn_bq': _L0_attn_in['bq'], 'L0_attn_Wk': _L0_attn_in['Wk'], 'L0_attn_bk': _L0_attn_in['bk'], 'L0_attn_Wv': _L0_attn_in['Wv'], 'L0_attn_bv': _L0_attn_in['bv'], 'L0_attn_q_scale': _L0_attn_in['q_scale'], 'L0_attn_q_bias': _L0_attn_in['q_bias'], 'L0_attn_k_scale': _L0_attn_in['k_scale'], 'L0_attn_k_bias': _L0_attn_in['k_bias'], 'L0_attn_v_scale': _L0_attn_in['v_scale'], 'L0_attn_v_bias': _L0_attn_in['v_bias'], 'L0_attn_Wo': _L0_attn_in['Wo'], 'L0_attn_bo': _L0_attn_in['bo'], 'L0_ffn_w_gate': _L0_ffn_in['w_gate'], 'L0_ffn_w_up': _L0_ffn_in['w_up'], 'L0_ffn_w_down': _L0_ffn_in['w_down']}
    _x0 = _d['L0_attn_x']
    _d['L0_attn_x'] = jax.random.normal(jax.random.fold_in(jax.random.key(seed), 1), (8, 512, 128), dtype=_x0.dtype)
    del _x0
    return _d

def reference(L0_attn_x, L0_attn_Wq, L0_attn_bq, L0_attn_Wk, L0_attn_bk, L0_attn_Wv, L0_attn_bv, L0_attn_q_scale, L0_attn_q_bias, L0_attn_k_scale, L0_attn_k_bias, L0_attn_v_scale, L0_attn_v_bias, L0_attn_Wo, L0_attn_bo, L0_ffn_w_gate, L0_ffn_w_up, L0_ffn_w_down):

    def _L0_attn_ref(x, Wq, bq, Wk, bk, Wv, bv, q_scale, q_bias, k_scale, k_bias, v_scale, v_bias, Wo, bo):
        import jax, jax.numpy as jnp
        import numpy as np
        B, S, H, NH = (2, 256, 128, 16)
        HD = H // NH
        EPS = 1e-06

        def _layernorm(x, scale, bias):
            x32 = x.astype(jnp.float32)
            mean = jnp.mean(x32, axis=-1, keepdims=True)
            var = jnp.mean(jnp.square(x32 - mean), axis=-1, keepdims=True)
            return (x32 - mean) * jax.lax.rsqrt(var + EPS) * scale + bias
        b, s, _ = x.shape
        q = (x @ Wq + bq).reshape(b, s, NH, HD)
        k = (x @ Wk + bk).reshape(b, s, NH, HD)
        v = (x @ Wv + bv).reshape(b, s, NH, HD)
        q = _layernorm(q, q_scale, q_bias)
        k = _layernorm(k, k_scale, k_bias)
        v = _layernorm(v, v_scale, v_bias)
        scale = HD ** (-0.5)
        scores = jnp.einsum('bqhd,bkhd->bhqk', q, k) * scale
        probs = jax.nn.softmax(scores, axis=-1)
        out = jnp.einsum('bhqk,bkhd->bqhd', probs, v).reshape(b, s, NH * HD)
        return out @ Wo + bo

    def _L0_ffn_ref(x, w_gate, w_up, w_down):
        import jax, jax.numpy as jnp
        import numpy as np
        DIM = 128
        HIDDEN = 384
        SCALE = 1.0 / 127.0

        def _dequant(w_int, dtype):
            return w_int.astype(dtype) * jnp.asarray(SCALE, dtype)
        wg = _dequant(w_gate, x.dtype)
        wu = _dequant(w_up, x.dtype)
        wd = _dequant(w_down, x.dtype)
        gate = jnp.einsum('bsd,hd->bsh', x, wg)
        up = jnp.einsum('bsd,hd->bsh', x, wu)
        h = jax.nn.silu(gate) * up
        return jnp.einsum('bsh,dh->bsd', h, wd)
    x = L0_attn_x
    x = x + _L0_attn_ref(_layernorm(x, axis=-1), L0_attn_Wq, L0_attn_bq, L0_attn_Wk, L0_attn_bk, L0_attn_Wv, L0_attn_bv, L0_attn_q_scale, L0_attn_q_bias, L0_attn_k_scale, L0_attn_k_bias, L0_attn_v_scale, L0_attn_v_bias, L0_attn_Wo, L0_attn_bo)
    x = x + _L0_ffn_ref(_layernorm(x, axis=-1), L0_ffn_w_gate, L0_ffn_w_up, L0_ffn_w_down)
    return x

_drawn_inputs = setup_inputs


def setup_inputs(seed=0):
    import zlib

    import numpy as np

    out = dict(_drawn_inputs(seed))
    spreads = {'L0_attn_bq': (0.0, 0.528),
     'L0_attn_bk': (0.0, 0.795),
     'L0_attn_bv': (0.0, 0.1),
     'L0_attn_q_scale': (1.0, 0.2),
     'L0_attn_q_bias': (0.0, 0.622),
     'L0_attn_k_scale': (1.0, 0.6),
     'L0_attn_k_bias': (0.0, 0.8),
     'L0_attn_v_scale': (1.0, 0.2),
     'L0_attn_v_bias': (0.0, 0.1),
     'L0_attn_bo': (0.0, 0.1)}
    factors = {}
    for name, (base, spread) in spreads.items():
        noise = np.random.default_rng([zlib.crc32(name.encode()), seed]).standard_normal(out[name].shape)
        drawn = base * np.exp(spread * noise) if base else spread * noise
        out[name] = jnp.asarray(drawn.astype(out[name].dtype))
    for name, factor in factors.items():
        out[name] = (out[name] * factor).astype(out[name].dtype)
    return out
```

```python
import numpy as np
import concourse.bass as bass
from concourse import mybir
from contextlib import ExitStack

F32 = mybir.dt.float32
BF16 = mybir.dt.bfloat16
I32 = mybir.dt.int32
ALU = mybir.AluOpType
ACT = mybir.ActivationFunctionType
AX = mybir.AxisListType

B, S, D = 8, 512, 128
NH, HD = 16, 8
HID = 384
P = 128
NT = S // P
NF = HID // P
NG = 4
NU = NG * NT
PAIRS = NH // 2
STRIP = 32
PART_ROWS = 6 * HD
SHIFT_ROWS = 2
ROWS = PART_ROWS + SHIFT_ROWS
HALF = 64
LN_EPS, HEAD_EPS = 1e-5, 1e-6
W_SCALE = float(np.float32(1.0 / 127.0))
SCORE_BOUND = 60.0
RSQRT_SEED = float(0x5F3759DF)
RUNS = [(0, (0, 0, 0), (0, 1, 2)), (3, (1, 1), (0, 1)), (5, (2,), (0,))]
PREP_REP, PREP_WT, PREP_BO, PREP_INT, PREP_ALL = 2, 3, 6, 12, 15
STACK_DMAS = 2 * 2
PART_DMAS = 2 * len(RUNS)

SIDE = {1: ["a_xT"], 2: ["b_OT3", "a_q"], 3: ["b_onT", "a_k"], 4: ["b_Wo", "a_v"], 5: ["a_var"],
        6: ["c_OT0"], 7: ["b_x2T", "a_rq", "a_rk"], 8: ["b_g0", "b_u0"], 9: ["b_g1"], 10: ["b_u1", "c_OT1"],
        11: ["b_g2", "b_u2"], 13: ["b_d0"], 14: ["b_d1", "c_OT2"]}
BANK = {"a_xT": 0, "b_OT3": 1, "a_q": 2, "b_onT": 0, "a_k": 1, "b_Wo": 2, "a_v": 0, "a_var": 1, "c_OT0": 2,
        "b_x2T": 0, "a_rq": 1, "a_rk": 2, "b_g0": 0, "b_u0": 1, "b_g1": 2, "b_u1": 0, "c_OT1": 1, "b_g2": 2,
        "b_u2": 0, "b_d0": 1, "c_OT2": 2}
SIDE_ORDER = [p for u in range(NU) for p in SIDE.get(u, []) if p != "b_d1"]
PHASE_PIECES = {
    "before": [p for p in SIDE_ORDER if p[0] == "a"],
    "first": [p for p in SIDE_ORDER if p[0] != "b"],
    "loop": SIDE_ORDER,
    "last": [p for p in SIDE_ORDER if p[0] != "a"],
    "after": [p for p in SIDE_ORDER if p[0] == "b"],
}


def sequence_of(piece, i):
    return {"a": i + 1, "b": i - 1, "c": i}[piece[0]]


def occupants_before(phase, i, piece):
    def same_bank(p):
        return BANK[p] == BANK[piece]
    own = [p for p in PHASE_PIECES[phase] if same_bank(p)]
    k = own.index(piece)
    if k:
        return [(own[k - 1], sequence_of(own[k - 1], i))]
    before = {"before": [], "first": ["before"], "loop": ["first", "loop"], "last": ["loop"], "after": ["last"]}
    lasts = {[p for p in PHASE_PIECES[ph] if same_bank(p)][-1] for ph in before[phase]}
    return [(p, sequence_of(p, i - 1)) for p in sorted(lasts)]


def at_least(eng, sem, value):
    if not (isinstance(value, int) and value <= 0):
        eng.wait_ge(sem, value)


def wait_apart(eng, sem, value, passed):
    at_least(eng, sem, value)
    eng.sem_inc(passed, 1)


def build(nc, x_d, Wq_d, bq_d, Wk_d, bk_d, Wv_d, bv_d, qs_d, qb_d, ks_d, kb_d, vs_d, vb_d, Wo_d, bo_d,
          wg_d, wu_d, wd_d, parts_d, maxes_d, out_d):
    ctx = ExitStack()
    with ctx:
        def sb(name, shape, dt=F32):
            return ctx.enter_context(nc.sbuf_tensor(name, shape, dt))

        def ps(name, shape, dt=F32):
            return ctx.enter_context(nc.psum_tensor(name, shape, dt))

        def sem(name):
            return ctx.enter_context(nc.semaphore(name))

        ident = sb("ident", [P, P])
        group8 = sb("group8", [P, P])
        center = sb("center", [P, P])
        wraw = sb("wraw", [P, 3, D])
        wrawT = sb("wrawT", [P, 3, D])
        wqkv = sb("wqkv", [P, 3, D])
        bias_col = sb("bias_col", [P, 3])
        bias_cen = sb("bias_cen", [P, 2])
        bv_rep = sb("bv_rep", [P, P])
        bv_row = sb("bv_row", [P, D])
        affine = sb("affine", [P, 6])
        q_aff = sb("q_aff", [P, 2])
        vb_rep = sb("vb_rep", [P, P])
        wo_raw = sb("wo_raw", [P, D])
        wo = sb("wo", [P, D])
        bo_row = sb("bo_row", [P, D])
        bo2_row = sb("bo2_row", [P, D])
        wg_i = sb("wg_i", [P, NF, D], I32)
        wu_i = sb("wu_i", [P, NF, D], I32)
        wd_i = sb("wd_i", [P, NF, D], I32)
        wg_f = sb("wg_f", [P, NF, D])
        wu_f = sb("wu_f", [P, NF, D])
        wd_f = sb("wd_f", [P, NF, D])
        wgT = sb("wgT", [P, NF, P])
        wuT = sb("wuT", [P, NF, P])
        wdT = sb("wdT", [P, NF, P])
        neg_half = sb("neg_half", [P, NT])
        prm = sb("prm", [1, 4, HD])
        prm2 = sb("prm2", [1, 4, HD])
        bnd = sb("bnd", [1, 8])
        flag = sb("flag", [1, 1], I32)

        x_in = sb("x_in", [P, NT, D])
        stats1 = sb("stats1", [P, NT, 6])
        mv1 = sb("mv1", [P, NT, 2])
        ve1 = sb("ve1", [P, NT])
        rs1 = sb("rs1", [P, NT])
        xn = sb("xn", [P, NT, D])
        xnT = sb("xnT", [P, S])
        qk_c = sb("qk_c", [P, 2, S])
        qk_sq = sb("qk_sq", [P, 2, S])
        v_c = sb("v_c", [P, NT, D])
        v_sq = sb("v_sq", [P, NT, D])
        v_sum = sb("v_sum", [P, NT * NH])
        hv = sb("hv", [P, 3, NT, NH])
        hy = sb("hy", [P, 3, NT, NH])
        ht = sb("ht", [P, 3, NT, NH])
        hyx = sb("hyx", [P, 2, NT, NH, HD])
        qk_n = sb("qk_n", [P, 2, S])
        qk_f = sb("qk_f", [P, 2, S])
        qk_r = sb("qk_r", [P, 2, S])
        parts = sb("parts", [P, 3, 2, S], BF16)
        qst = sb("qst", [P, PAIRS, 2, S], BF16)
        kst = sb("kst", [P, PAIRS, S], BF16)
        vaug = sb("vaug", [P, NT, NH, STRIP])
        probs = sb("probs", [P, NT, NG, S])
        osb = sb("osb", [P, S])
        rinv = sb("rinv", [P, NT, NG])
        on = sb("on", [P, NT, D])
        mx = sb("mx", [P, NH, NT])
        mx_hi = sb("mx_hi", [NH * NT, P], BF16)
        mx_lo = sb("mx_lo", [NH * NT, P], BF16)
        x_res = sb("x_res", [P, NT, D])
        x_bo = sb("x_bo", [P, NT, D])
        onT = sb("onT", [P, S])
        x2 = sb("x2", [P, NT, D])
        stats2 = sb("stats2", [P, NT, 6])
        mv2 = sb("mv2", [P, NT, 2])
        ve2 = sb("ve2", [P, NT])
        rs2 = sb("rs2", [P, NT])
        x2n = sb("x2n", [P, NT, D])
        x2T = sb("x2T", [P, S])
        th = sb("th", [P, NF, S])
        ga = sb("ga", [P, NF, S])
        hT = sb("hT", [P, NF, S])
        y = sb("y", [P, NT, D])

        scores = ps("scores", [P, 4, S])
        oacc = ps("oacc", [P, S])
        side = ps("side", [P, 3, S])

        w_loaded = sem("w_loaded")
        wi_loaded = sem("wi_loaded")
        x_loaded = sem("x_loaded")
        xres_loaded = sem("xres_loaded")
        parts_stored = sem("parts_stored")
        stackA_loaded = sem("stackA_loaded")
        stackB_loaded = sem("stackB_loaded")
        out_stored = sem("out_stored")
        maxes_stored = sem("maxes_stored")
        shift_loaded = sem("shift_loaded")
        passed = sem("passed")
        filled = sem("filled")
        consts = sem("consts")
        prep_v = sem("prep_v")
        prep_t = sem("prep_t")
        bound_step = sem("bound_step")
        flag_ready = sem("flag_ready")
        stacks_init = sem("stacks_init")
        stats1_done = sem("stats1_done")
        mv1_done = sem("mv1_done")
        ve1_done = sem("ve1_done")
        rs1_done = sem("rs1_done")
        xn_done = sem("xn_done")
        xT_filled = sem("xT_filled")
        xnT_done = sem("xnT_done")
        q_filled = sem("q_filled")
        k_filled = sem("k_filled")
        v_filled = sem("v_filled")
        qkc_done = sem("qkc_done")
        vc_done = sem("vc_done")
        vsq_done = sem("vsq_done")
        vsum_done = sem("vsum_done")
        qksq_done = sem("qksq_done")
        var_filled = sem("var_filled")
        hv_done = sem("hv_done")
        seed_done = sem("seed_done")
        newton = sem("newton")
        rsqrt_done = sem("rsqrt_done")
        r_filled = sem("r_filled")
        qkn_done = sem("qkn_done")
        qkf_done = sem("qkf_done")
        part1_done = sem("part1_done")
        rest1_done = sem("rest1_done")
        part2_done = sem("part2_done")
        part3_done = sem("part3_done")
        vaugA_done = sem("vaugA_done")
        vaugB_done = sem("vaugB_done")
        qk_done = sem("qk_done")
        exp_done = sem("exp_done")
        pv_done = sem("pv_done")
        osb_done = sem("osb_done")
        OT_filled = sem("OT_filled")
        rinv_done = sem("rinv_done")
        on_done = sem("on_done")
        mx_filled = sem("mx_filled")
        mx_taken = sem("mx_taken")
        mxT_filled = sem("mxT_filled")
        mx_parts = sem("mx_parts")
        onT_filled = sem("onT_filled")
        onT_done = sem("onT_done")
        xbo_done = sem("xbo_done")
        Wo_filled = sem("Wo_filled")
        x2_done = sem("x2_done")
        stats2_done = sem("stats2_done")
        mv2_done = sem("mv2_done")
        ve2_done = sem("ve2_done")
        rs2_done = sem("rs2_done")
        x2n_done = sem("x2n_done")
        x2T_filled = sem("x2T_filled")
        x2T_done = sem("x2T_done")
        g_filled = sem("g_filled")
        u_filled = sem("u_filled")
        tanh_done = sem("tanh_done")
        ga_done = sem("ga_done")
        h_done = sem("h_done")
        d_filled = sem("d_filled")
        y_done = sem("y_done")
        read_out = {"xT": (xnT_done, 1, 0), "q": (qkc_done, 2, 0), "k": (qkc_done, 2, 1), "v": (vc_done, 1, 0),
                    "var": (hv_done, 2, 0), "rq": (qkn_done, 2, 0), "rk": (qkn_done, 2, 1),
                    "onT": (onT_done, 1, 0), "Wo": (x2_done, 1, 0), "x2T": (x2T_done, 1, 0), "d0": (y_done, 1, 0)}
        read_out.update({f"OT{g}": (on_done, NG, g) for g in range(NG)})
        read_out.update({f"g{j}": (ga_done, NF, j) for j in range(NF)})
        read_out.update({f"u{j}": (h_done, NF, j) for j in range(NF)})

        x_t = x_d.rearrange("b (p t) d -> b p t d", t=NT)
        out_t = out_d.rearrange("b (p t) d -> b p t d", t=NT)
        head_vec = [qs_d, qb_d, ks_d, kb_d, vs_d, vb_d]
        N_W = 3 + 3 + 6 + 2 + 4

        block = ctx.enter_context(nc.Block())

        @block.sync
        def _(sp):
            def load_x(b):
                if not (isinstance(b, int) and b == 0):
                    wait_apart(sp, xn_done, NT * b, passed)
                sp.dma_start(x_in[:, :, :], x_t[b, :, :, :]).then_inc(x_loaded, 16)

            def store_parts(b):
                wait_apart(sp, part3_done, b + 1, passed)
                if not (isinstance(b, int) and b == 0):
                    wait_apart(sp, stackB_loaded, 16 * STACK_DMAS * b, passed)
                for which in range(2):
                    for slot, q_parts, k_parts in RUNS:
                        run = (q_parts, k_parts)[which]
                        n = len(run)
                        if n > 1 and run[0] == run[1]:
                            src = parts[:, run[0]:run[0] + 1, which, :].broadcast_to((P, n, S))
                        else:
                            src = parts[:, run[0]:run[0] + n, which, :]
                        sp.dma_start(parts_d[which, :, slot:slot + n, :], src).then_inc(parts_stored, 16)

            def load_stack(b, half, loaded):
                wait_apart(sp, parts_stored, 16 * PART_DMAS * (b + 1), passed)
                if not (isinstance(b, int) and b == 0):
                    wait_apart(sp, qk_done, 2 * NU * b - (NU if half == 0 else 0), passed)
                for parity in range(2):
                    for which, stack in ((0, qst[:, :, parity, :]), (1, kst[:, :, :])):
                        r0 = HALF * parity
                        src = parts_d[which].rearrange("(c z d) r s -> z (d r) c s", z=2, d=HD)[parity]
                        sp.dma_start(stack[r0:r0 + PART_ROWS, 4 * half:4 * half + 4, :],
                                     src[:, 4 * half:4 * half + 4, :]).then_inc(loaded, 16)

            def load_res(b):
                wait_apart(sp, xbo_done, b, passed)
                sp.dma_start(x_res[:, :, :], x_t[b, :, :, :]).then_inc(xres_loaded, 16)

            def store_out(b):
                wait_apart(sp, y_done, b + 1, passed)
                sp.dma_start(out_t[b, :, :, :], y[:, :, :]).then_inc(out_stored, 16)

            def shift_rows(i):
                sp.wait_ge(mx_parts, 2 * (i + 1))
                for part, src in enumerate((mx_hi, mx_lo)):
                    sp.dma_start(maxes_d[part].rearrange("h t p -> (h t) p"), src[:, :])\
                      .then_inc(maxes_stored, 16)
                sp.wait_ge(maxes_stored, 32 * (i + 1))
                for parity in range(2):
                    r0 = HALF * parity + PART_ROWS
                    sp.dma_start(qst[r0:r0 + 2, :, parity, :],
                                 maxes_d.rearrange("r (c z) t p -> z r c (t p)", z=2)[parity])\
                      .then_inc(shift_loaded, 16)

            load_x(0)
            for dst, src in ((wg_i, wg_d.rearrange("(j p) d -> p j d", p=P)),
                             (wu_i, wu_d.rearrange("(j p) d -> p j d", p=P)),
                             (wd_i, wd_d.rearrange("p (j h) -> p j h", j=NF))):
                sp.dma_start(dst[:, :, :], src).then_inc(wi_loaded, 16)
            load_x(1)
            load_res(0)
            sp.wait_ge(stacks_init, 2)
            store_parts(0)
            load_stack(0, 0, stackA_loaded)
            sp.wait_ge(flag_ready, 1)
            needs_max = sp.value_load(flag[0:1, 0:1], min_val=0, max_val=1)

            def turn(i, phase):
                load_stack(i, 1, stackB_loaded)
                with sp.If(needs_max > 0):
                    shift_rows(i)
                if not (isinstance(i, int) and i + 2 >= B):
                    load_x(i + 2)
                if phase in ("first", "loop"):
                    store_parts(i + 1)
                    load_stack(i + 1, 0, stackA_loaded)
                if phase in ("loop", "last"):
                    load_res(i)
                    store_out(i - 1)

            turn(0, "first")
            turn(1, "loop")
            with sp.Fori(2, B - 2) as i:
                turn(i, "loop")
            turn(B - 2, "loop")
            turn(B - 1, "last")
            store_out(B - 1)
            sp.wait_ge(out_stored, 16 * B)
            sp.wait_ge(parts_stored, 16 * PART_DMAS * B)
            with sp.If(needs_max > 0):
                sp.wait_ge(maxes_stored, 32 * B)

        @block.gpsimd
        def _(pool):
            pool.memset(ident[:, :], 0.0).then_inc(filled, 1)
            pool.memset(group8[:, :], 1.0 / HD).then_inc(filled, 1)
            pool.memset(neg_half[:, :], -0.5).then_inc(filled, 1)
            pool.wait_ge(filled, 3)
            pool.affine_select(out=ident[:, :], in_=ident[:, :], compare_op=ALU.not_equal, fill=1.0, base=0,
                               pattern=[[-1, P]], channel_multiplier=1).then_inc(filled, 1)
            blocks = group8[:, :].rearrange("p (h d) -> p h d", d=HD)
            pool.affine_select(out=blocks, in_=blocks, compare_op=ALU.is_ge, fill=0.0, base=0,
                               pattern=[[-HD, NH], [0, HD]], channel_multiplier=1).then_inc(filled, 1)
            pool.wait_ge(filled, 5)
            pool.affine_select(out=blocks, in_=blocks, compare_op=ALU.is_ge, fill=0.0, base=HD - 1,
                               pattern=[[HD, NH], [0, HD]], channel_multiplier=-1).then_inc(filled, 1)
            pool.wait_ge(filled, 6)
            pool.tensor_tensor(out=center[:, :], in0=ident[:, :], in1=group8[:, :], op=ALU.subtract)\
                .then_inc(consts, 1)
            pool.memset(vaug[:, :, :, HD:STRIP], 0.0).then_inc(filled, 1)
            pool.wait_ge(filled, 7)
            pool.memset(vaug[:, :, :, HD:HD + 1], 1.0).then_inc(consts, 1)

            def norm_power(b, mv, ve, rs, mv_done, ve_done, rs_done):
                wait_apart(pool, mv_done, NT * (b + 1), passed)
                pool.tensor_scalar(ve[:, :], mv[:, :, 1], LN_EPS, None, ALU.add).then_inc(ve_done, 1)
                pool.wait_ge(ve_done, b + 1)
                pool.tensor_tensor(out=rs[:, :], in0=ve[:, :], in1=neg_half[:, :], op=ALU.pow).then_inc(rs_done, 1)

            def squares(b):
                for w in range(2):
                    pool.wait_ge(qkc_done, 2 * b + w + 1)
                    pool.tensor_tensor(out=qk_sq[:, w, :], in0=qk_c[:, w, :], in1=qk_c[:, w, :], op=ALU.mult)\
                        .then_inc(qksq_done, 1)
                pool.wait_ge(vc_done, b + 1)
                pool.tensor_tensor(out=v_sq[:, :, :], in0=v_c[:, :, :], in1=v_c[:, :, :], op=ALU.mult)\
                    .then_inc(vsq_done, 1)

            def split(b):
                pool.wait_ge(part1_done, b + 1)
                pool.tensor_tensor(out=qk_r[:, :, :], in0=qk_f[:, :, :], in1=parts[:, 0, :, :], op=ALU.subtract)\
                    .then_inc(rest1_done, 1)
                pool.wait_ge(part2_done, b + 1)
                pool.tensor_tensor(out=parts[:, 2, :, :], in0=qk_r[:, :, :], in1=parts[:, 1, :, :], op=ALU.subtract)\
                    .then_inc(part3_done, 1)

            def residual(b):
                pool.wait_ge(xres_loaded, 16 * (b + 1))
                at_least(pool, x2_done, b)
                pool.tensor_tensor(out=x_bo[:, :, :], in0=x_res[:, :, :],
                                   in1=bo2_row[:, :].unsqueeze(1).broadcast_to((P, NT, D)), op=ALU.add)\
                    .then_inc(xbo_done, 1)

            norm_power(0, mv1, ve1, rs1, mv1_done, ve1_done, rs1_done)
            squares(0)
            split(0)
            pool.wait_ge(prep_v, PREP_BO)

            def turn(i, phase):
                if phase in ("first", "loop"):
                    norm_power(i + 1, mv1, ve1, rs1, mv1_done, ve1_done, rs1_done)
                if phase != "first":
                    residual(i - 1)
                if phase in ("first", "loop"):
                    squares(i + 1)
                if phase != "first":
                    norm_power(i - 1, mv2, ve2, rs2, mv2_done, ve2_done, rs2_done)
                if phase in ("first", "loop"):
                    split(i + 1)

            turn(0, "first")
            turn(1, "loop")
            with pool.Fori(2, B - 1) as i:
                turn(i, "loop")
            turn(B - 1, "last")
            residual(B - 1)
            norm_power(B - 1, mv2, ve2, rs2, mv2_done, ve2_done, rs2_done)

        @block.scalar
        def _(act):
            for k, src in enumerate((Wq_d, Wk_d, Wv_d)):
                act.dma_start(wraw[:, k, :], src).then_inc(w_loaded, 16)
            for k, src in enumerate((bq_d, bk_d, bv_d)):
                act.dma_start(bias_col[:, k:k + 1], src.rearrange("(p a) -> p a", a=1)).then_inc(w_loaded, 16)
            for k, src in enumerate(head_vec):
                act.dma_start(affine[:, k:k + 1],
                              src.rearrange("(a d b) -> a d b", a=1, b=1).broadcast_to((NH, HD, 1)))\
                   .then_inc(w_loaded, 16)
            act.dma_start(wo_raw[:, :], Wo_d).then_inc(w_loaded, 16)
            act.dma_start(bo_row[:, :], bo_d.rearrange("(a n) -> a n", a=1).broadcast_to((P, D)))\
               .then_inc(w_loaded, 16)
            for k, src in enumerate(head_vec[:4]):
                act.dma_start(prm[:, k, :], src.rearrange("(a n) -> a n", a=1)).then_inc(w_loaded, 16)

            def tanh(b, j, bank):
                act.wait_ge(g_filled, NF * b + j + 1)
                act.activation(th[:, j, :], side[:, bank, :], ACT.Tanh, scale=0.5).then_inc(tanh_done, 1)

            def copy_o(b, g):
                act.wait_ge(pv_done, NU * b + NT * (g + 1))
                at_least(act, OT_filled, NG * b + g)
                act.activation(osb[:, :], oacc[:, :], ACT.Copy).then_inc(osb_done, 1)

            TANH_AT = {8: 0, 9: 1, 11: 2}

            def turn(i, phase):
                for u in range(NU):
                    kt = u % NT
                    at_least(act, pv_done, NU * i + u - NT + 1)
                    for c in range(2):
                        act.wait_ge(qk_done, 2 * NU * i + 2 * u + c + 1)
                        act.activation(probs[:, kt, 2 * c:2 * c + 2, :], scores[:, 2 * c:2 * c + 2, :], ACT.Exp)\
                           .then_inc(exp_done, 1)
                        if c == 0 and u % NT == 1 and (u > 1 or phase != "first"):
                            copy_o(i if u > 1 else i - 1, (u // NT - 1) % NG)
                    if phase != "first" and u in TANH_AT:
                        j = TANH_AT[u]
                        tanh(i - 1, j, BANK[f"b_g{j}"])

            turn(0, "first")
            turn(1, "loop")
            with act.Fori(2, B - 1) as i:
                turn(i, "loop")
            turn(B - 1, "last")
            copy_o(B - 1, NG - 1)
            for j in range(NF):
                tanh(B - 1, j, BANK[f"b_g{j}"])

        @block.tensor
        def _(pe):
            pe.wait_ge(filled, 4)
            pe.wait_ge(consts, 1)
            pe.wait_ge(w_loaded, 16 * N_W)
            for k in range(3):
                last = pe.transpose(side[:, 0, k * D:(k + 1) * D], wraw[:, k, :], ident[:, :])
            last.then_inc(prep_t, 1)
            for k in range(2):
                last = pe.matmul(side[:, 1, k:k + 1], center[:, :], bias_col[:, k:k + 1], start=True, stop=True)
            pe.wait_ge(prep_v, PREP_REP)
            pe.matmul(side[:, 1, D:2 * D], bv_rep[:, :], center[:, :], start=True, stop=True)
            last = pe.matmul(side[:, 1, 2 * D:3 * D], vb_rep[:, :], wo_raw[:, :], start=True, stop=True)
            last.then_inc(prep_t, 1)
            pe.wait_ge(prep_v, PREP_WT)
            for k in range(3):
                last = pe.matmul(side[:, 0, k * D:(k + 1) * D], wrawT[:, k, :], center[:, :], start=True, stop=True)
            last.then_inc(prep_t, 1)
            for m, w in enumerate((wg_f, wu_f, wd_f)):
                pe.wait_ge(prep_v, PREP_INT + m)
                for j in range(NF):
                    last = pe.transpose(side[:, m % 2, j * P:(j + 1) * P], w[:, j, :], ident[:, :])
                last.then_inc(prep_t, 1)
            pe.wait_ge(prep_v, PREP_ALL)

            def bank_free(phase, i, piece):
                for p, b in occupants_before(phase, i, piece):
                    done, per_sequence, place = read_out[p[2:]]
                    at_least(pe, done, per_sequence * b + place + 1)
                return side[:, BANK[piece], :]

            def transposes(dst, src):
                for t in range(NT):
                    last = pe.transpose(dst[:, t * P:(t + 1) * P], src(t), ident[:, :])
                return last

            def piece(name, phase, i):
                what = name[2:]
                b = sequence_of(name, i)
                if name != "b_d1":
                    bank = bank_free(phase, i, name)
                else:
                    bank = side[:, BANK["b_d0"], :]
                if what == "xT":
                    pe.wait_ge(xn_done, NT * (b + 1))
                    transposes(bank, lambda t: xn[:, t, :]).then_inc(xT_filled, 1)
                elif what in ("q", "k"):
                    pe.wait_ge(xnT_done, b + 1)
                    w = 0 if what == "q" else 1
                    pe.matmul(bank, wqkv[:, w, :], xnT[:, :], start=True, stop=True)\
                      .then_inc(q_filled if what == "q" else k_filled, 1)
                elif what == "v":
                    pe.wait_ge(xnT_done, b + 1)
                    for t in range(NT):
                        last = pe.matmul(bank[:, t * D:(t + 1) * D], xnT[:, t * P:(t + 1) * P], wqkv[:, 2, :],
                                         start=True, stop=True)
                    last.then_inc(v_filled, 1)
                elif what == "var":
                    pe.wait_ge(qksq_done, 2 * (b + 1))
                    for w in range(2):
                        for t in range(NT):
                            o = (w * NT + t) * NH
                            last = pe.matmul(bank[:, o:o + NH], qk_sq[:, w, t * P:(t + 1) * P],
                                             group8[:, 0:P:HD], start=True, stop=True)
                    last.then_inc(var_filled, 1)
                elif what in ("rq", "rk"):
                    pe.wait_ge(rsqrt_done, 2 * (b + 1))
                    w = 0 if what == "rq" else 1
                    transposes(bank, lambda t: hyx[:, w, t, :, :])\
                        .then_inc(r_filled, 1)
                elif what[:2] == "OT":
                    g = int(what[2])
                    pe.wait_ge(osb_done, NG * b + g + 1)
                    transposes(bank, lambda t: osb[:, t * P:(t + 1) * P]).then_inc(OT_filled, 1)
                elif what == "onT":
                    pe.wait_ge(on_done, NG * (b + 1))
                    transposes(bank, lambda t: on[:, t, :]).then_inc(onT_filled, 1)
                elif what == "Wo":
                    pe.wait_ge(onT_done, b + 1)
                    for t in range(NT):
                        last = pe.matmul(bank[:, t * D:(t + 1) * D], onT[:, t * P:(t + 1) * P], wo[:, :],
                                         start=True, stop=True)
                    last.then_inc(Wo_filled, 1)
                elif what == "x2T":
                    pe.wait_ge(x2n_done, NT * (b + 1))
                    transposes(bank, lambda t: x2n[:, t, :]).then_inc(x2T_filled, 1)
                elif what[0] in "gu":
                    j = int(what[1])
                    pe.wait_ge(x2T_done, b + 1)
                    pe.matmul(bank, (wgT if what[0] == "g" else wuT)[:, j, :], x2T[:, :], start=True, stop=True)\
                      .then_inc(g_filled if what[0] == "g" else u_filled, 1)
                else:
                    pe.wait_ge(h_done, NF * (b + 1))
                    half = int(what[1])
                    for t in (2 * half, 2 * half + 1):
                        for j in range(NF):
                            last = pe.matmul(bank[:, t * D:(t + 1) * D], hT[:, j, t * P:(t + 1) * P], wdT[:, j, :],
                                             start=(j == 0), stop=(j == NF - 1))
                    if half == 1:
                        last.then_inc(d_filled, 1)

            def scores_of(i, u, c):
                g, kt = u // NT, u % NT
                at_least(pe, exp_done, 2 * NU * i + 2 * u + c - 1)
                pair = 2 * g + c
                for parity in range(2):
                    last = pe.matmul(scores[:, 2 * c + parity, :], kst[:, pair, kt * P:(kt + 1) * P],
                                     qst[:, pair, parity, :], start=True, stop=True)
                last.then_inc(qk_done, 1)

            def times_v(i, n):
                g, kt = (n % NU) // NT, n % NT
                at_least(pe, exp_done, 2 * NU * i + 2 * n + 2)
                if n % NU in (0, NU // 2):
                    pe.wait_ge(vaugA_done if n % NU == 0 else vaugB_done, i + 1)
                if kt == 0:
                    at_least(pe, osb_done, NG * i + g)
                for j in range(NG):
                    last = pe.matmul(oacc[STRIP * j:STRIP * (j + 1), :], vaug[:, kt, NG * g + j, :],
                                     probs[:, kt, j, :], start=(kt == 0), stop=(kt == NT - 1))
                last.then_inc(pv_done, 1)

            def row_max_scores(i):
                for h in range(NH):
                    parity, pair = h % 2, h // 2
                    r = slice(HALF * parity, HALF * parity + PART_ROWS)
                    for t in range(NT):
                        n = NT * h + t
                        at_least(pe, mx_taken, NH * NT * i + n - 3 if n >= 4 else NH * NT * i)
                        pe.matmul(scores[:, n % 4, :], qst[r, pair, parity, t * P:(t + 1) * P], kst[r, pair, :],
                                  start=True, stop=True).then_inc(mx_filled, 1)
                wait_apart(pe, mx_taken, NH * NT * (i + 1), passed)
                pe.transpose(scores[0:NH * NT, 0, 0:P], mx[:, :, :], ident[:, :]).then_inc(mxT_filled, 1)
                pe.wait_ge(shift_loaded, 32 * (i + 1))

            pe.wait_ge(flag_ready, 1)
            needs_max = pe.value_load(flag[0:1, 0:1], min_val=0, max_val=1)
            for name in PHASE_PIECES["before"]:
                piece(name, "before", -1)

            def turn(i, phase):
                pe.wait_ge(stackA_loaded, 16 * STACK_DMAS * (i + 1))
                at_least(pe, exp_done, 2 * NU * i)
                with pe.If(needs_max > 0):
                    pe.wait_ge(stackB_loaded, 16 * STACK_DMAS * (i + 1))
                    row_max_scores(i)
                for u in range(NU):
                    if u == NU // 2:
                        pe.wait_ge(stackB_loaded, 16 * STACK_DMAS * (i + 1))
                    todo = [p for p in SIDE.get(u, []) if p == "b_d1" and phase != "first" or p in PHASE_PIECES[phase]]
                    scores_of(i, u, 0)
                    if u >= 2 or phase != "first":
                        times_v(i, u - 2)
                    scores_of(i, u, 1)
                    for name in todo:
                        piece(name, phase, i)

            turn(0, "first")
            turn(1, "loop")
            with pe.Fori(2, B - 1) as i:
                turn(i, "loop")
            turn(B - 1, "last")
            times_v(B, -2)
            times_v(B, -1)
            for name in PHASE_PIECES["after"]:
                piece(name, "after", B)
                if name == "b_d0":
                    piece("b_d1", "after", B)

        @block.vector
        def _(dve):
            dve.memset(qst[:, :, :, :], 0.0).then_inc(stacks_init, 1)
            dve.memset(kst[:, :, :], 1.0).then_inc(stacks_init, 1)
            n_prep = [0]

            def prep(ins):
                n_prep[0] += 1
                ins.then_inc(prep_v, 1)
                return n_prep[0]
            dve.wait_ge(w_loaded, 16 * N_W)
            prep(dve.tensor_copy(bv_rep[:, :], bias_col[:, 2:3].broadcast_to((P, P))))
            assert prep(dve.tensor_copy(vb_rep[:, :], affine[:, 5:6].broadcast_to((P, P)))) == PREP_REP
            dve.wait_ge(prep_t, 1)
            assert prep(dve.tensor_copy(wrawT[:, :, :], side[:, 0, 0:3 * D].rearrange("p (k d) -> p k d", k=3)))\
                == PREP_WT
            dve.wait_ge(prep_t, 2)
            prep(dve.tensor_copy(bias_cen[:, :], side[:, 1, 0:2]))
            prep(dve.tensor_copy(bv_row[:, :], side[:, 1, D:2 * D]))
            assert prep(dve.tensor_tensor(out=bo2_row[:, :], in0=side[:, 1, 2 * D:3 * D], in1=bo_row[:, :],
                                          op=ALU.add)) == PREP_BO
            prep(dve.tensor_scalar(q_aff[:, :], affine[:, 0:2], HD ** -0.5, None, ALU.mult))
            prep(dve.tensor_scalar(wo[:, :], wo_raw[:, :], affine[:, 4:5], None, ALU.mult))
            dve.wait_ge(wi_loaded, 48)
            dve.tensor_scalar(wu_f[:, :, :], wu_i[:, :, :], W_SCALE, None, ALU.mult).then_inc(prep_v, 1)
            dve.tensor_scalar(wd_f[:, :, :], wd_i[:, :, :], W_SCALE, 0.5, ALU.mult, ALU.mult).then_inc(prep_v, 1)
            dve.tensor_scalar(wg_f[:, :, :], wg_i[:, :, :], W_SCALE, None, ALU.mult).then_inc(prep_v, 1)
            n_prep[0] += 3
            dve.wait_ge(prep_t, 3)
            assert prep(dve.tensor_copy(wqkv[:, :, :], side[:, 0, 0:3 * D].rearrange("p (k d) -> p k d", k=3)))\
                == PREP_INT
            for m, wT in enumerate((wgT, wuT, wdT)):
                dve.wait_ge(prep_t, 4 + m)
                prep(dve.tensor_copy(wT[:, :, :], side[:, m % 2, 0:NF * P].rearrange("p (j d) -> p j d", j=NF)))
            assert n_prep[0] == PREP_ALL

            steps = [0]

            def link(ins):
                steps[0] += 1
                ins.then_inc(bound_step, 1)
                dve.wait_ge(bound_step, steps[0])
            link(dve.tensor_tensor(out=prm2[:, :, :], in0=prm[:, :, :], in1=prm[:, :, :], op=ALU.mult))
            link(dve.reduce_max(bnd[:, 0:2], prm2[:, 0:4:2, :], AX.X))
            link(dve.reduce_sum(bnd[:, 2:4], prm2[:, 1:4:2, :], AX.X))
            link(dve.scalar_tensor_tensor(out=bnd[:, 4:6], in0=bnd[:, 0:2], scalar=float(HD), in1=bnd[:, 2:4],
                                          op0=ALU.mult, op1=ALU.add))
            link(dve.tensor_tensor(out=bnd[:, 6:7], in0=bnd[:, 4:5], in1=bnd[:, 5:6], op=ALU.mult))
            link(dve.tensor_scalar(bnd[:, 7:8], bnd[:, 6:7], SCORE_BOUND ** 2 * HD / 4, -1.0, ALU.is_le, ALU.mult))
            dve.tensor_scalar(flag[:, :], bnd[:, 7:8], 1.0, None, ALU.add).then_inc(flag_ready, 1)

            def norm_stats(b, src, stats, mv, src_ready, stats_done, mv_done):
                src_ready()
                for t in range(NT):
                    dve.bn_stats(stats[:, t, :], src[:, t, :]).then_inc(stats_done, 1)
                for t in range(NT):
                    wait_apart(dve, stats_done, NT * b + t + 1, passed)
                    dve.bn_aggr(mv[:, t, :], stats[:, t, :]).then_inc(mv_done, 1)

            def norm_apply(b, src, dst, mv, rs, rs_done, done):
                dve.wait_ge(rs_done, b + 1)
                for t in range(NT):
                    dve.tensor_scalar(dst[:, t, :], src[:, t, :], mv[:, t, 0:1], rs[:, t:t + 1],
                                      ALU.subtract, ALU.mult).then_inc(done, 1)

            def ln1(b):
                norm_stats(b, x_in, stats1, mv1, lambda: dve.wait_ge(x_loaded, 16 * (b + 1)), stats1_done, mv1_done)
                norm_apply(b, x_in, xn, mv1, rs1, rs1_done, xn_done)

            def copy_xT(b):
                dve.wait_ge(xT_filled, b + 1)
                dve.tensor_copy(xnT[:, :], side[:, BANK["a_xT"], :])\
                   .then_inc(xnT_done, 1)

            def centred(b, w):
                name, sem_f = (("a_q", q_filled), ("a_k", k_filled))[w]
                dve.wait_ge(sem_f, b + 1)
                dve.tensor_scalar(qk_c[:, w, :], side[:, BANK[name], :], bias_cen[:, w:w + 1], None, ALU.add)\
                   .then_inc(qkc_done, 1)

            def centred_v(b):
                dve.wait_ge(v_filled, b + 1)
                at_least(dve, vaugB_done, b)
                dve.tensor_tensor(out=v_c[:, :, :],
                                  in0=side[:, BANK["a_v"], :].rearrange("p (t d) -> p t d", t=NT),
                                  in1=bv_row[:, :].unsqueeze(1).broadcast_to((P, NT, D)), op=ALU.add)\
                   .then_inc(vc_done, 1)

            def variances(b):
                dve.wait_ge(vsq_done, b + 1)
                dve.reduce_sum(v_sum[:, :], v_sq[:, :, :].rearrange("p t (h d) -> p (t h) d", d=HD), AX.X)\
                   .then_inc(vsum_done, 1)
                dve.wait_ge(var_filled, b + 1)
                dve.tensor_scalar(hv[:, 0:2, :, :].rearrange("p w t h -> p (w t h)"),
                                  side[:, BANK["a_var"], 0:2 * NT * NH], HEAD_EPS, None, ALU.add)\
                   .then_inc(hv_done, 1)
                dve.wait_ge(vsum_done, b + 1)
                dve.tensor_scalar(hv[:, 2, :, :].rearrange("p t h -> p (t h)"), v_sum[:, :], 1.0 / HD, HEAD_EPS,
                                  ALU.mult, ALU.add).then_inc(hv_done, 1)
                dve.wait_ge(hv_done, 2 * (b + 1))
                dve.tensor_scalar(hy[:, :, :, :].bitcast(I32), hv[:, :, :, :].bitcast(I32), -0.5, RSQRT_SEED,
                                  ALU.mult, ALU.add).then_inc(seed_done, 1)
                dve.wait_ge(seed_done, b + 1)
                n = [0]
                STEPS = 8
                flat = "p w t h -> p (w t h)"
                v_all, y_all, t_all = (z[:, :, :, :].rearrange(flat) for z in (hv, hy, ht))

                def step(ins):
                    n[0] += 1
                    ins.then_inc(newton, 1)
                    dve.wait_ge(newton, STEPS * b + n[0])
                for k in range(3):
                    step(dve.tensor_tensor(out=t_all, in0=y_all, in1=y_all, op=ALU.mult))
                    step(dve.scalar_tensor_tensor(out=t_all, in0=t_all, scalar=-0.5, in1=v_all,
                                                  op0=ALU.mult, op1=ALU.mult))
                    if k < 2:
                        step(dve.scalar_tensor_tensor(out=y_all, in0=t_all, scalar=1.5, in1=y_all,
                                                      op0=ALU.add, op1=ALU.mult))
                nqk = 2 * NT * NH
                dve.scalar_tensor_tensor(out=hyx[:, :, :, :, :].rearrange("p w t h d -> p (w t h) d"),
                                         in0=t_all[:, 0:nqk].unsqueeze(2).broadcast_to((P, nqk, HD)), scalar=1.5,
                                         in1=y_all[:, 0:nqk].unsqueeze(2).broadcast_to((P, nqk, HD)),
                                         op0=ALU.add, op1=ALU.mult).then_inc(rsqrt_done, 1)
                dve.scalar_tensor_tensor(out=y_all[:, nqk:], in0=t_all[:, nqk:], scalar=1.5, in1=y_all[:, nqk:],
                                         op0=ALU.add, op1=ALU.mult).then_inc(rsqrt_done, 1)

            def normed(b):
                dve.wait_ge(r_filled, 2 * (b + 1))
                for w, name in enumerate(("a_rq", "a_rk")):
                    dve.tensor_tensor(out=qk_n[:, w, :], in0=side[:, BANK[name], :], in1=qk_c[:, w, :], op=ALU.mult)\
                       .then_inc(qkn_done, 1)
                for w in range(2):
                    sc, bi = ((q_aff[:, 0:1], q_aff[:, 1:2]), (affine[:, 2:3], affine[:, 3:4]))[w]
                    dve.wait_ge(qkn_done, 2 * b + w + 1)
                    dve.tensor_scalar(qk_f[:, w, :], qk_n[:, w, :], sc, bi, ALU.mult, ALU.add).then_inc(qkf_done, 1)
                at_least(dve, parts_stored, 16 * PART_DMAS * b)
                dve.wait_ge(qkf_done, 2 * (b + 1))
                dve.tensor_copy(parts[:, 0, :, :], qk_f[:, :, :]).then_inc(part1_done, 1)

            def second_part(b):
                dve.wait_ge(rest1_done, b + 1)
                dve.tensor_copy(parts[:, 1, :, :], qk_r[:, :, :]).then_inc(part2_done, 1)

            def fill_v(b, half):
                at_least(dve, pv_done, NU * b - (NU // 2 if half == 0 else 0))
                if half == 0:
                    dve.wait_ge(rsqrt_done, 2 * (b + 1))
                hh = NH // 2
                for t in range(NT):
                    v = v_c[:, t, :].rearrange("p (h d) -> p h d", d=HD)[:, hh * half:hh * (half + 1), :]
                    last = dve.tensor_tensor(out=vaug[:, t, hh * half:hh * (half + 1), 0:HD], in0=v,
                                             in1=hy[:, 2, t, hh * half:hh * (half + 1)].unsqueeze(2)
                                             .broadcast_to((P, hh, HD)), op=ALU.mult)
                last.then_inc(vaugA_done if half == 0 else vaugB_done, 1)

            def divide(b, g):
                name = ("c_OT0", "c_OT1", "c_OT2", "b_OT3")[g]
                o = side[:, BANK[name], :].rearrange("p (t j x) -> p t j x", t=NT, j=NG)
                dve.wait_ge(OT_filled, NG * b + g + 1)
                if g == 0:
                    at_least(dve, onT_filled, b)
                at_least(dve, on_done, NG * b + g)
                dve.reciprocal(rinv[:, :, :], o[:, :, :, HD]).then_inc(rinv_done, 1)
                dve.wait_ge(rinv_done, NG * b + g + 1)
                dve.tensor_tensor(out=on[:, :, g * NG * HD:(g + 1) * NG * HD].rearrange("p t (j d) -> p t j d", d=HD),
                                  in0=o[:, :, :, 0:HD],
                                  in1=rinv[:, :, :].unsqueeze(3).broadcast_to((P, NT, NG, HD)), op=ALU.mult)\
                   .then_inc(on_done, 1)

            def copy_onT(b):
                dve.wait_ge(onT_filled, b + 1)
                dve.tensor_copy(onT[:, :], side[:, BANK["b_onT"], :])\
                   .then_inc(onT_done, 1)

            def ln2_stats(b):
                dve.wait_ge(Wo_filled, b + 1)
                dve.wait_ge(xbo_done, b + 1)
                dve.tensor_tensor(out=x2[:, :, :], in0=side[:, BANK["b_Wo"], :].rearrange("p (t d) -> p t d", t=NT),
                                  in1=x_bo[:, :, :], op=ALU.add).then_inc(x2_done, 1)
                norm_stats(b, x2, stats2, mv2, lambda: dve.wait_ge(x2_done, b + 1), stats2_done, mv2_done)

            def ln2_apply(b):
                norm_apply(b, x2, x2n, mv2, rs2, rs2_done, x2n_done)

            def copy_x2T(b):
                dve.wait_ge(x2T_filled, b + 1)
                dve.tensor_copy(x2T[:, :], side[:, BANK["b_x2T"], :])\
                   .then_inc(x2T_done, 1)

            def silu_up(b, j):
                dve.wait_ge(tanh_done, NF * b + j + 1)
                dve.scalar_tensor_tensor(out=ga[:, j, :], in0=th[:, j, :], scalar=1.0, in1=side[:, BANK[f"b_g{j}"], :],
                                         op0=ALU.add, op1=ALU.mult)\
                   .then_inc(ga_done, 1)
                dve.wait_ge(u_filled, NF * b + j + 1)
                dve.wait_ge(ga_done, NF * b + j + 1)
                dve.tensor_tensor(out=hT[:, j, :], in0=side[:, BANK[f"b_u{j}"], :], in1=ga[:, j, :], op=ALU.mult)\
                   .then_inc(h_done, 1)

            def result(b):
                dve.wait_ge(d_filled, b + 1)
                at_least(dve, out_stored, 16 * b)
                dve.tensor_tensor(out=y[:, :, :], in0=side[:, BANK["b_d0"], :].rearrange("p (t d) -> p t d", t=NT),
                                  in1=x2[:, :, :], op=ALU.add).then_inc(y_done, 1)

            def row_maxima(i):
                for n in range(NH * NT):
                    dve.wait_ge(mx_filled, NH * NT * i + n + 1)
                    dve.tensor_reduce(out=mx[:, n // NT, n % NT:n % NT + 1], in_=scores[:, n % 4, :], axis=AX.X,
                                      op=ALU.max, negate=True).then_inc(mx_taken, 1)
                dve.wait_ge(mxT_filled, i + 1)
                at_least(dve, maxes_stored, 32 * i)
                dve.tensor_copy(mx_hi[:, :], scores[0:NH * NT, 0, 0:P]).then_inc(mx_parts, 1)
                dve.wait_ge(mx_parts, 2 * i + 1)
                dve.tensor_tensor(out=mx_lo[:, :], in0=scores[0:NH * NT, 0, 0:P], in1=mx_hi[:, :], op=ALU.subtract)\
                   .then_inc(mx_parts, 1)

            ln1(0)
            copy_xT(0)
            centred(0, 0)
            centred(0, 1)
            centred_v(0)
            variances(0)
            normed(0)
            second_part(0)
            dve.wait_ge(consts, 2)
            fill_v(0, 0)
            dve.wait_ge(flag_ready, 1)
            needs_max = dve.value_load(flag[0:1, 0:1], min_val=0, max_val=1)

            def turn(i, phase):
                ahead = phase in ("first", "loop")
                behind = phase != "first"
                with dve.If(needs_max > 0):
                    row_maxima(i)
                if ahead:
                    ln1(i + 1)
                    copy_xT(i + 1)
                fill_v(i, 1)
                if behind:
                    divide(i - 1, 3)
                if ahead:
                    centred(i + 1, 0)
                if behind:
                    copy_onT(i - 1)
                if ahead:
                    centred(i + 1, 1)
                if behind:
                    ln2_stats(i - 1)
                if ahead:
                    centred_v(i + 1)
                    variances(i + 1)
                if behind:
                    ln2_apply(i - 1)
                divide(i, 0)
                if behind:
                    copy_x2T(i - 1)
                if ahead:
                    normed(i + 1)
                if behind:
                    silu_up(i - 1, 0)
                if ahead:
                    second_part(i + 1)
                if behind:
                    silu_up(i - 1, 1)
                divide(i, 1)
                if ahead:
                    fill_v(i + 1, 0)
                if behind:
                    silu_up(i - 1, 2)
                    result(i - 1)
                divide(i, 2)

            turn(0, "first")
            turn(1, "loop")
            with dve.Fori(2, B - 1) as i:
                turn(i, "loop")
            turn(B - 1, "last")
            divide(B - 1, 3)
            copy_onT(B - 1)
            ln2_stats(B - 1)
            ln2_apply(B - 1)
            copy_x2T(B - 1)
            for j in range(NF):
                silu_up(B - 1, j)
            result(B - 1)


INPUTS = ["L0_attn_x", "L0_attn_Wq", "L0_attn_bq", "L0_attn_Wk", "L0_attn_bk", "L0_attn_Wv", "L0_attn_bv",
          "L0_attn_q_scale", "L0_attn_q_bias", "L0_attn_k_scale", "L0_attn_k_bias", "L0_attn_v_scale",
          "L0_attn_v_bias", "L0_attn_Wo", "L0_attn_bo", "L0_ffn_w_gate", "L0_ffn_w_up", "L0_ffn_w_down"]


def kernel(**inputs):
    from concourse import bacc
    from concourse.bass_utils import run_bass_kernel_spmd

    nc = bacc.Bacc("TRN2", target_bir_lowering=False, num_devices=1)
    arrays, args = {}, []
    for name in INPUTS:
        a = np.ascontiguousarray(inputs[name])
        arrays["in_" + name] = a
        args.append(nc.dram_tensor("in_" + name, a.shape, mybir.dt.from_np(a.dtype), kind="ExternalInput").ap())
    parts = nc.dram_tensor("parts_dram", (2, P, 6, S), BF16, kind="Internal").ap()
    maxes = nc.dram_tensor("maxes_dram", (2, NH, NT, P), BF16, kind="Internal").ap()
    out = nc.dram_tensor("out_dram", (B, S, D), F32, kind="ExternalOutput").ap()
    build(nc, *args, parts, maxes, out)
    r = run_bass_kernel_spmd(nc, [arrays], core_ids=[0])
    return r.results[0]["out_dram"]
```

```python
import numpy as np
import concourse.bass as bass
from concourse import mybir
from contextlib import ExitStack

F32 = mybir.dt.float32
BF16 = mybir.dt.bfloat16
I32 = mybir.dt.int32
ALU = mybir.AluOpType
ACT = mybir.ActivationFunctionType
AX = mybir.AxisListType

B, S, D = 8, 512, 128
NH, HD = 16, 8
HID = 384
P = 128
NT = S // P
NF = HID // P
NG = 4
NU = NG * NT
PAIRS = NH // 2
STRIP = 32
HC = HD + 1
NO = 2
PART_ROWS = 6 * HD
SHIFT_ROWS = 2
ROWS = PART_ROWS + SHIFT_ROWS
HALF = 64
LN_EPS, HEAD_EPS = 1e-5, 1e-6
W_SCALE = float(np.float32(1.0 / 127.0))
SCORE_BOUND = 60.0
RSQRT_SEED = float(0x5F3759DF)
PLACES = [[(0, 0, 1, 3), (1, 0, 3, 2), (1, 5, 1, 1)], [(0, 3, 1, 2), (1, 1, 3, 2)], [(0, 5, 1, 1), (1, 2, 1, 1)]]
PREP_REP, PREP_WT, PREP_QKV, PREP_INT, PREP_ALL = 1, 2, 5, 11, 15
STACK_DMAS = 2 * 2
PART_DMAS = sum(len(p) for p in PLACES)

SIDE = {1: ["a_xT"], 2: ["b_OT1", "a_q"], 3: ["b_onT", "a_k"], 4: ["b_Wo", "a_v"], 5: ["a_var"],
        6: ["b_x2T"], 7: ["b_g0"], 8: ["a_rq", "a_rk"], 9: ["b_u0", "b_g1"], 10: ["b_u1", "c_OT0"],
        11: ["b_g2", "b_u2"], 13: ["b_d0"], 14: ["b_d1"]}
BANK = {"a_xT": 0, "b_OT1": 1, "a_q": 2, "b_onT": 0, "a_k": 1, "b_Wo": 2, "a_v": 0, "a_var": 1,
        "b_x2T": 2, "b_g0": 0, "a_rq": 1, "a_rk": 2, "b_u0": 1, "b_g1": 2, "b_u1": 0, "c_OT0": 1, "b_g2": 2,
        "b_u2": 0, "b_d0": 1}
SIDE_ORDER = [p for u in range(NU) for p in SIDE.get(u, []) if p != "b_d1"]
PHASE_PIECES = {
    "before": [p for p in SIDE_ORDER if p[0] == "a"],
    "first": [p for p in SIDE_ORDER if p[0] != "b"],
    "loop": SIDE_ORDER,
    "last": [p for p in SIDE_ORDER if p[0] != "a"],
    "after": [p for p in SIDE_ORDER if p[0] == "b"],
}


def sequence_of(piece, i):
    return {"a": i + 1, "b": i - 1, "c": i}[piece[0]]


def occupants_before(phase, i, piece):
    def same_bank(p):
        return BANK[p] == BANK[piece]
    own = [p for p in PHASE_PIECES[phase] if same_bank(p)]
    k = own.index(piece)
    if k:
        return [(own[k - 1], sequence_of(own[k - 1], i))]
    before = {"before": [], "first": ["before"], "loop": ["first", "loop"], "last": ["loop"], "after": ["last"]}
    lasts = {[p for p in PHASE_PIECES[ph] if same_bank(p)][-1] for ph in before[phase]}
    return [(p, sequence_of(p, i - 1)) for p in sorted(lasts)]


def at_least(eng, sem, value):
    if not (isinstance(value, int) and value <= 0):
        eng.wait_ge(sem, value)


def wait_apart(eng, sem, value, passed):
    at_least(eng, sem, value)
    eng.sem_inc(passed, 1)


def build(nc, x_d, Wq_d, bq_d, Wk_d, bk_d, Wv_d, bv_d, qs_d, qb_d, ks_d, kb_d, vs_d, vb_d, Wo_d, bo_d,
          wg_d, wu_d, wd_d, parts_d, maxes_d, out_d):
    ctx = ExitStack()
    with ctx:
        def sb(name, shape, dt=F32):
            return ctx.enter_context(nc.sbuf_tensor(name, shape, dt))

        def ps(name, shape, dt=F32):
            return ctx.enter_context(nc.psum_tensor(name, shape, dt))

        def sem(name):
            return ctx.enter_context(nc.semaphore(name))

        ident = sb("ident", [P, P])
        group8 = sb("group8", [P, P])
        center = sb("center", [P, P])
        wraw = sb("wraw", [P, 3, D])
        wrawT = sb("wrawT", [P, 3, D])
        wqkv = sb("wqkv", [P, 3, D])
        bias_col = sb("bias_col", [P, 3])
        bias_cen = sb("bias_cen", [P, 2])
        bv_rep = sb("bv_rep", [P, P])
        bv_row = sb("bv_row", [P, D])
        affine = sb("affine", [P, 6])
        q_aff = sb("q_aff", [P, 2])
        vb_rep = sb("vb_rep", [P, P])
        wo_raw = sb("wo_raw", [P, D])
        wo = sb("wo", [P, D])
        bo_row = sb("bo_row", [P, D])
        bo2_row = sb("bo2_row", [P, D])
        wg_i = sb("wg_i", [P, NF, D], I32)
        wu_i = sb("wu_i", [P, NF, D], I32)
        wd_i = sb("wd_i", [P, NF, D], I32)
        wg_f = sb("wg_f", [P, NF, D])
        wu_f = sb("wu_f", [P, NF, D])
        wd_f = sb("wd_f", [P, NF, D])
        wgT = sb("wgT", [P, NF, P])
        wuT = sb("wuT", [P, NF, P])
        wdT = sb("wdT", [P, NF, P])
        neg_half = sb("neg_half", [P, NT])
        prm = sb("prm", [1, 4, HD])
        prm2 = sb("prm2", [1, 4, HD])
        bnd = sb("bnd", [1, 8])
        flag = sb("flag", [1, 1], I32)

        x_in = sb("x_in", [P, NT, D])
        stats1 = sb("stats1", [P, NT, 6])
        mv1 = sb("mv1", [P, NT, 2])
        ve1 = sb("ve1", [P, NT])
        rs1 = sb("rs1", [P, NT])
        xn = sb("xn", [P, NT, D])
        xnT = sb("xnT", [P, S])
        qk_c = sb("qk_c", [P, 2, S])
        qk_sq = sb("qk_sq", [P, 2, S])
        v_c = sb("v_c", [P, NT, D])
        v_sq = sb("v_sq", [P, NT, D])
        v_sum = sb("v_sum", [P, NT * NH])
        hv = sb("hv", [P, 3, NT, NH])
        hy = sb("hy", [P, 3, NT, NH])
        ht = sb("ht", [P, 3, NT, NH])
        hyx = sb("hyx", [P, 2, NT, NH, HD])
        qk_n = sb("qk_n", [P, 2, S])
        qk_f = sb("qk_f", [P, 2, S])
        qk_r = sb("qk_r", [P, 2, S])
        parts = sb("parts", [P, 3, 2, S], BF16)
        qst = sb("qst", [P, PAIRS, 2, S], BF16)
        kst = sb("kst", [P, PAIRS, S], BF16)
        vaug = sb("vaug", [P, NT, NH, STRIP])
        probs = sb("probs", [P, NT, NG, S])
        osb = sb("osb", [P, S])
        rinv = sb("rinv", [P, 2, NT, NG])
        on = sb("on", [P, NT, D])
        mx = sb("mx", [P, NH, NT])
        mx_hi = sb("mx_hi", [NH * NT, P], BF16)
        mx_lo = sb("mx_lo", [NH * NT, P], BF16)
        x_res = sb("x_res", [P, NT, D])
        x_bo = sb("x_bo", [P, NT, D])
        onT = sb("onT", [P, S])
        x2 = sb("x2", [P, NT, D])
        stats2 = sb("stats2", [P, NT, 6])
        mv2 = sb("mv2", [P, NT, 2])
        ve2 = sb("ve2", [P, NT])
        rs2 = sb("rs2", [P, NT])
        x2n = sb("x2n", [P, NT, D])
        x2T = sb("x2T", [P, S])
        th = sb("th", [P, NF, S])
        ga = sb("ga", [P, NF, S])
        hT = sb("hT", [P, NF, S])
        y = sb("y", [P, NT, D])

        scores = ps("scores", [P, 4, S])
        oacc = ps("oacc", [P, S])
        side = ps("side", [P, 3, S])

        w_loaded = sem("w_loaded")
        wi_loaded = sem("wi_loaded")
        aux_loaded = sem("aux_loaded")
        x_loaded = sem("x_loaded")
        xres_loaded = sem("xres_loaded")
        parts_stored = sem("parts_stored")
        stackA_loaded = sem("stackA_loaded")
        stackB_loaded = sem("stackB_loaded")
        out_stored = sem("out_stored")
        maxes_stored = sem("maxes_stored")
        shift_loaded = sem("shift_loaded")
        passed = sem("passed")
        filled = sem("filled")
        consts = sem("consts")
        prep_v = sem("prep_v")
        prep_t = sem("prep_t")
        bound_step = sem("bound_step")
        flag_ready = sem("flag_ready")
        stacks_init = sem("stacks_init")
        stats1_done = sem("stats1_done")
        mv1_done = sem("mv1_done")
        ve1_done = sem("ve1_done")
        rs1_done = sem("rs1_done")
        xn_done = sem("xn_done")
        xT_filled = sem("xT_filled")
        xnT_done = sem("xnT_done")
        q_filled = sem("q_filled")
        k_filled = sem("k_filled")
        v_filled = sem("v_filled")
        qkc_done = sem("qkc_done")
        vc_done = sem("vc_done")
        vsq_done = sem("vsq_done")
        vsum_done = sem("vsum_done")
        qksq_done = sem("qksq_done")
        var_filled = sem("var_filled")
        hv_done = sem("hv_done")
        seed_done = sem("seed_done")
        newton = sem("newton")
        rsqrt_done = sem("rsqrt_done")
        r_filled = sem("r_filled")
        qkn_done = sem("qkn_done")
        qkf_done = sem("qkf_done")
        part_done = sem("part_done")
        rest_done = sem("rest_done")
        vaugA_done = sem("vaugA_done")
        vaugB_done = sem("vaugB_done")
        qk_done = sem("qk_done")
        exp_done = sem("exp_done")
        pv_done = sem("pv_done")
        osb_done = sem("osb_done")
        OT_filled = sem("OT_filled")
        rinv_done = sem("rinv_done")
        on_done = sem("on_done")
        mx_filled = sem("mx_filled")
        mx_taken = sem("mx_taken")
        mxT_filled = sem("mxT_filled")
        mx_parts = sem("mx_parts")
        onT_filled = sem("onT_filled")
        onT_done = sem("onT_done")
        xbo_done = sem("xbo_done")
        Wo_filled = sem("Wo_filled")
        x2_done = sem("x2_done")
        stats2_done = sem("stats2_done")
        mv2_done = sem("mv2_done")
        ve2_done = sem("ve2_done")
        rs2_done = sem("rs2_done")
        x2n_done = sem("x2n_done")
        x2T_filled = sem("x2T_filled")
        x2T_done = sem("x2T_done")
        g_filled = sem("g_filled")
        u_filled = sem("u_filled")
        tanh_done = sem("tanh_done")
        ga_done = sem("ga_done")
        h_done = sem("h_done")
        d_filled = sem("d_filled")
        y_done = sem("y_done")
        read_out = {"xT": (xnT_done, 1, 0), "q": (qkc_done, 2, 0), "k": (qkc_done, 2, 1), "v": (vc_done, 1, 0),
                    "var": (hv_done, 2, 0), "rq": (qkn_done, 2, 0), "rk": (qkn_done, 2, 1),
                    "onT": (onT_done, 1, 0), "Wo": (x2_done, 1, 0), "x2T": (x2T_done, 1, 0), "d0": (y_done, 1, 0)}
        read_out.update({f"OT{o}": (on_done, NO, o) for o in range(NO)})
        read_out.update({f"g{j}": (ga_done, NF, j) for j in range(NF)})
        read_out.update({f"u{j}": (h_done, NF, j) for j in range(NF)})

        x_t = x_d.rearrange("b (p t) d -> b p t d", t=NT)
        out_t = out_d.rearrange("b (p t) d -> b p t d", t=NT)
        head_vec = [qs_d, qb_d, ks_d, kb_d, vs_d, vb_d]
        N_W, N_AUX = 3 + 3, 4 + 6 + 2

        block = ctx.enter_context(nc.Block())

        @block.sync
        def _(sp):
            def load_x(b):
                if not (isinstance(b, int) and b == 0):
                    wait_apart(sp, xn_done, NT * b, passed)
                sp.dma_start(x_in[:, :, :], x_t[b, :, :, :]).then_inc(x_loaded, 16)

            def store_parts(b):
                if not (isinstance(b, int) and b == 0):
                    wait_apart(sp, stackB_loaded, 16 * STACK_DMAS * b, passed)
                for part, places in enumerate(PLACES):
                    wait_apart(sp, part_done, 3 * b + part + 1, passed)
                    for which, slot, step, n in places:
                        src = parts[:, part:part + 1, which, :]
                        sp.dma_start(parts_d[which, :, slot:slot + step * (n - 1) + 1:step, :],
                                     src if n == 1 else src.broadcast_to((P, n, S))).then_inc(parts_stored, 16)

            def load_stack(b, half, loaded):
                wait_apart(sp, parts_stored, 16 * PART_DMAS * (b + 1), passed)
                if not (isinstance(b, int) and b == 0):
                    wait_apart(sp, qk_done, 2 * NU * b - (NU if half == 0 else 0), passed)
                for parity in range(2):
                    for which, stack in ((0, qst[:, :, parity, :]), (1, kst[:, :, :])):
                        r0 = HALF * parity
                        src = parts_d[which].rearrange("(c z d) r s -> z (d r) c s", z=2, d=HD)[parity]
                        sp.dma_start(stack[r0:r0 + PART_ROWS, 4 * half:4 * half + 4, :],
                                     src[:, 4 * half:4 * half + 4, :]).then_inc(loaded, 16)

            def load_res(b):
                wait_apart(sp, xbo_done, b, passed)
                sp.dma_start(x_res[:, :, :], x_t[b, :, :, :]).then_inc(xres_loaded, 16)

            def store_out(b):
                wait_apart(sp, y_done, b + 1, passed)
                sp.dma_start(out_t[b, :, :, :], y[:, :, :]).then_inc(out_stored, 16)

            def shift_rows(i):
                sp.wait_ge(mx_parts, 2 * (i + 1))
                for part, src in enumerate((mx_hi, mx_lo)):
                    sp.dma_start(maxes_d[part].rearrange("h t p -> (h t) p"), src[:, :])\
                      .then_inc(maxes_stored, 16)
                sp.wait_ge(maxes_stored, 32 * (i + 1))
                for parity in range(2):
                    r0 = HALF * parity + PART_ROWS
                    sp.dma_start(qst[r0:r0 + 2, :, parity, :],
                                 maxes_d.rearrange("r (c z) t p -> z r c (t p)", z=2)[parity])\
                      .then_inc(shift_loaded, 16)

            load_x(0)
            for dst, src in ((wg_i, wg_d.rearrange("(j p) d -> p j d", p=P)),
                             (wu_i, wu_d.rearrange("(j p) d -> p j d", p=P)),
                             (wd_i, wd_d.rearrange("p (j h) -> p j h", j=NF))):
                sp.dma_start(dst[:, :, :], src).then_inc(wi_loaded, 16)
            load_x(1)
            load_res(0)
            sp.wait_ge(stacks_init, 2)
            store_parts(0)
            load_stack(0, 0, stackA_loaded)
            sp.wait_ge(flag_ready, 1)
            needs_max = sp.value_load(flag[0:1, 0:1], min_val=0, max_val=1)

            def turn(i, phase):
                load_stack(i, 1, stackB_loaded)
                with sp.If(needs_max > 0):
                    shift_rows(i)
                if not (isinstance(i, int) and i + 2 >= B):
                    load_x(i + 2)
                if phase in ("first", "loop"):
                    store_parts(i + 1)
                    load_stack(i + 1, 0, stackA_loaded)
                if phase in ("loop", "last"):
                    load_res(i)
                    store_out(i - 1)

            turn(0, "first")
            turn(1, "loop")
            with sp.Fori(2, B - 2) as i:
                turn(i, "loop")
            turn(B - 2, "loop")
            turn(B - 1, "last")
            store_out(B - 1)
            sp.wait_ge(out_stored, 16 * B)
            sp.wait_ge(parts_stored, 16 * PART_DMAS * B)
            with sp.If(needs_max > 0):
                sp.wait_ge(maxes_stored, 32 * B)

        @block.gpsimd
        def _(pool):
            pool.memset(ident[:, :], 0.0).then_inc(filled, 1)
            pool.memset(group8[:, :], 1.0 / HD).then_inc(filled, 1)
            pool.memset(neg_half[:, :], -0.5).then_inc(filled, 1)
            pool.wait_ge(filled, 3)
            pool.affine_select(out=ident[:, :], in_=ident[:, :], compare_op=ALU.not_equal, fill=1.0, base=0,
                               pattern=[[-1, P]], channel_multiplier=1).then_inc(filled, 1)
            blocks = group8[:, :].rearrange("p (h d) -> p h d", d=HD)
            pool.affine_select(out=blocks, in_=blocks, compare_op=ALU.is_ge, fill=0.0, base=0,
                               pattern=[[-HD, NH], [0, HD]], channel_multiplier=1).then_inc(filled, 1)
            pool.wait_ge(filled, 5)
            pool.affine_select(out=blocks, in_=blocks, compare_op=ALU.is_ge, fill=0.0, base=HD - 1,
                               pattern=[[HD, NH], [0, HD]], channel_multiplier=-1).then_inc(filled, 1)
            pool.wait_ge(filled, 6)
            pool.tensor_tensor(out=center[:, :], in0=ident[:, :], in1=group8[:, :], op=ALU.subtract)\
                .then_inc(consts, 1)
            def norm_power(b, mv, ve, rs, mv_done, ve_done, rs_done):
                wait_apart(pool, mv_done, NT * (b + 1), passed)
                pool.tensor_scalar(ve[:, :], mv[:, :, 1], LN_EPS, None, ALU.add).then_inc(ve_done, 1)
                pool.wait_ge(ve_done, b + 1)
                pool.tensor_tensor(out=rs[:, :], in0=ve[:, :], in1=neg_half[:, :], op=ALU.pow).then_inc(rs_done, 1)

            def v_squares(b):
                pool.wait_ge(vc_done, b + 1)
                pool.tensor_tensor(out=v_sq[:, :, :], in0=v_c[:, :, :], in1=v_c[:, :, :], op=ALU.mult)\
                    .then_inc(vsq_done, 1)

            def residual(b):
                pool.wait_ge(xres_loaded, 16 * (b + 1))
                at_least(pool, x2_done, b)
                pool.tensor_tensor(out=x_bo[:, :, :], in0=x_res[:, :, :],
                                   in1=bo2_row[:, :].unsqueeze(1).broadcast_to((P, NT, D)), op=ALU.add)\
                    .then_inc(xbo_done, 1)

            norm_power(0, mv1, ve1, rs1, mv1_done, ve1_done, rs1_done)
            pool.memset(vaug[:, :, :, :], 0.0).then_inc(filled, 1)
            pool.wait_ge(filled, 7)
            for k in range(2):
                ones = vaug[:, :, :, HC * k + HD].rearrange("p t (o k j) -> p k (t o) j", k=2, j=NG)[:, k, :, :]
                pool.memset(ones, 1.0).then_inc(consts, 1)

            pool.memset(qst[:, :, :, :].bitcast(I32), 0).then_inc(stacks_init, 1)
            pool.memset(kst[:, :, :], 1.0).then_inc(stacks_init, 1)
            v_squares(0)
            pool.wait_ge(prep_v, PREP_ALL)

            def turn(i, phase):
                if phase in ("first", "loop"):
                    norm_power(i + 1, mv1, ve1, rs1, mv1_done, ve1_done, rs1_done)
                if phase != "first":
                    residual(i - 1)
                if phase != "first":
                    norm_power(i - 1, mv2, ve2, rs2, mv2_done, ve2_done, rs2_done)
                if phase in ("first", "loop"):
                    v_squares(i + 1)

            turn(0, "first")
            turn(1, "loop")
            with pool.Fori(2, B - 1) as i:
                turn(i, "loop")
            turn(B - 1, "last")
            residual(B - 1)
            norm_power(B - 1, mv2, ve2, rs2, mv2_done, ve2_done, rs2_done)

        @block.scalar
        def _(act):
            for k, src in enumerate((Wq_d, Wk_d, Wv_d)):
                act.dma_start(wraw[:, k, :], src).then_inc(w_loaded, 16)
            for k, src in enumerate((bq_d, bk_d, bv_d)):
                act.dma_start(bias_col[:, k:k + 1], src.rearrange("(p a) -> p a", a=1)).then_inc(w_loaded, 16)
            for k, src in enumerate(head_vec[:4]):
                act.dma_start(prm[:, k, :], src.rearrange("(a n) -> a n", a=1)).then_inc(aux_loaded, 16)
            for k, src in enumerate(head_vec):
                act.dma_start(affine[:, k:k + 1],
                              src.rearrange("(a d b) -> a d b", a=1, b=1).broadcast_to((NH, HD, 1)))\
                   .then_inc(aux_loaded, 16)
            act.dma_start(wo_raw[:, :], Wo_d).then_inc(aux_loaded, 16)
            act.dma_start(bo_row[:, :], bo_d.rearrange("(a n) -> a n", a=1).broadcast_to((P, D)))\
               .then_inc(aux_loaded, 16)

            def tanh(b, j, bank):
                act.wait_ge(g_filled, NF * b + j + 1)
                act.activation(th[:, j, :], side[:, bank, :], ACT.Tanh, scale=0.5).then_inc(tanh_done, 1)

            def copy_o(b, o):
                act.wait_ge(pv_done, NU * b + NU // NO * (o + 1))
                at_least(act, OT_filled, NO * b + o)
                act.activation(osb[:, :], oacc[:, :], ACT.Copy).then_inc(osb_done, 1)

            def squares(b):
                for w in range(2):
                    act.wait_ge(qkc_done, 2 * b + w + 1)
                    act.activation(qk_sq[:, w, :], qk_c[:, w, :], ACT.Square).then_inc(qksq_done, 1)

            squares(0)
            SQUARES_AT = 4
            TANH_AT = {7: 0, 9: 1, 11: 2}

            def turn(i, phase):
                for u in range(NU):
                    kt = u % NT
                    at_least(act, pv_done, NU * i + u - NT + 1)
                    for c in range(2):
                        act.wait_ge(qk_done, 2 * NU * i + 2 * u + c + 1)
                        act.activation(probs[:, kt, 2 * c:2 * c + 2, :], scores[:, 2 * c:2 * c + 2, :], ACT.Exp)\
                           .then_inc(exp_done, 1)
                        if c == 0 and u == 1 and phase != "first":
                            copy_o(i - 1, 1)
                        if c == 0 and u == NU // NO + 1:
                            copy_o(i, 0)
                    if phase in ("first", "loop") and u == SQUARES_AT:
                        squares(i + 1)
                    if phase != "first" and u in TANH_AT:
                        j = TANH_AT[u]
                        tanh(i - 1, j, BANK[f"b_g{j}"])

            turn(0, "first")
            turn(1, "loop")
            with act.Fori(2, B - 1) as i:
                turn(i, "loop")
            turn(B - 1, "last")
            copy_o(B - 1, 1)
            for j in range(NF):
                tanh(B - 1, j, BANK[f"b_g{j}"])

        @block.tensor
        def _(pe):
            pe.wait_ge(filled, 4)
            pe.wait_ge(consts, 1)
            pe.wait_ge(w_loaded, 16 * N_W)
            for k in range(3):
                last = pe.transpose(side[:, 0, k * D:(k + 1) * D], wraw[:, k, :], ident[:, :])
            last.then_inc(prep_t, 1)
            pe.wait_ge(prep_v, PREP_REP)
            for k in range(2):
                pe.matmul(side[:, 1, k:k + 1], center[:, :], bias_col[:, k:k + 1], start=True, stop=True)
            last = pe.matmul(side[:, 1, D:2 * D], bv_rep[:, :], center[:, :], start=True, stop=True)
            last.then_inc(prep_t, 1)
            pe.wait_ge(prep_v, PREP_WT)
            for k in range(3):
                last = pe.matmul(side[:, 0, k * D:(k + 1) * D], wrawT[:, k, :], center[:, :], start=True, stop=True)
            last.then_inc(prep_t, 1)
            pe.wait_ge(prep_v, PREP_QKV)

            def prepare_later_weights():
                pe.wait_ge(prep_v, PREP_INT)
                pe.wait_ge(vc_done, 1)
                pe.wait_ge(qkn_done, 2)
                pe.matmul(side[:, 0, NF * P:NF * P + D], vb_rep[:, :], wo_raw[:, :], start=True, stop=True)
                for m, w in enumerate((wg_f, wu_f, wd_f)):
                    for j in range(NF):
                        last = pe.transpose(side[:, m, j * P:(j + 1) * P], w[:, j, :], ident[:, :])
                    last.then_inc(prep_t, 1)
                pe.wait_ge(prep_v, PREP_ALL)

            def bank_free(phase, i, piece):
                for p, b in occupants_before(phase, i, piece):
                    done, per_sequence, place = read_out[p[2:]]
                    at_least(pe, done, per_sequence * b + place + 1)
                return side[:, BANK[piece], :]

            def transposes(dst, src):
                for t in range(NT):
                    last = pe.transpose(dst[:, t * P:(t + 1) * P], src(t), ident[:, :])
                return last

            def piece(name, phase, i):
                what = name[2:]
                b = sequence_of(name, i)
                if name != "b_d1":
                    bank = bank_free(phase, i, name)
                else:
                    bank = side[:, BANK["b_d0"], :]
                if what == "xT":
                    pe.wait_ge(xn_done, NT * (b + 1))
                    transposes(bank, lambda t: xn[:, t, :]).then_inc(xT_filled, 1)
                elif what in ("q", "k"):
                    pe.wait_ge(xnT_done, b + 1)
                    w = 0 if what == "q" else 1
                    pe.matmul(bank, wqkv[:, w, :], xnT[:, :], start=True, stop=True)\
                      .then_inc(q_filled if what == "q" else k_filled, 1)
                elif what == "v":
                    pe.wait_ge(xnT_done, b + 1)
                    for t in range(NT):
                        last = pe.matmul(bank[:, t * D:(t + 1) * D], xnT[:, t * P:(t + 1) * P], wqkv[:, 2, :],
                                         start=True, stop=True)
                    last.then_inc(v_filled, 1)
                elif what == "var":
                    pe.wait_ge(qksq_done, 2 * (b + 1))
                    for w in range(2):
                        for t in range(NT):
                            o = (w * NT + t) * NH
                            last = pe.matmul(bank[:, o:o + NH], qk_sq[:, w, t * P:(t + 1) * P],
                                             group8[:, 0:P:HD], start=True, stop=True)
                    last.then_inc(var_filled, 1)
                elif what in ("rq", "rk"):
                    pe.wait_ge(rsqrt_done, 2 * (b + 1))
                    w = 0 if what == "rq" else 1
                    transposes(bank, lambda t: hyx[:, w, t, :, :])\
                        .then_inc(r_filled, 1)
                elif what[:2] == "OT":
                    pe.wait_ge(osb_done, NO * b + int(what[2]) + 1)
                    transposes(bank, lambda t: osb[:, t * P:(t + 1) * P]).then_inc(OT_filled, 1)
                elif what == "onT":
                    pe.wait_ge(on_done, NO * (b + 1))
                    transposes(bank, lambda t: on[:, t, :]).then_inc(onT_filled, 1)
                elif what == "Wo":
                    pe.wait_ge(onT_done, b + 1)
                    for t in range(NT):
                        last = pe.matmul(bank[:, t * D:(t + 1) * D], onT[:, t * P:(t + 1) * P], wo[:, :],
                                         start=True, stop=True)
                    last.then_inc(Wo_filled, 1)
                elif what == "x2T":
                    pe.wait_ge(x2n_done, NT * (b + 1))
                    transposes(bank, lambda t: x2n[:, t, :]).then_inc(x2T_filled, 1)
                elif what[0] in "gu":
                    j = int(what[1])
                    pe.wait_ge(x2T_done, b + 1)
                    pe.matmul(bank, (wgT if what[0] == "g" else wuT)[:, j, :], x2T[:, :], start=True, stop=True)\
                      .then_inc(g_filled if what[0] == "g" else u_filled, 1)
                else:
                    pe.wait_ge(h_done, NF * (b + 1))
                    half = int(what[1])
                    for t in (2 * half, 2 * half + 1):
                        for j in range(NF):
                            last = pe.matmul(bank[:, t * D:(t + 1) * D], hT[:, j, t * P:(t + 1) * P], wdT[:, j, :],
                                             start=(j == 0), stop=(j == NF - 1))
                    if half == 1:
                        last.then_inc(d_filled, 1)

            def scores_of(i, u, c):
                g, kt = u // NT, u % NT
                at_least(pe, exp_done, 2 * NU * i + 2 * u + c - 1)
                pair = 2 * g + c
                for parity in range(2):
                    last = pe.matmul(scores[:, 2 * c + parity, :], kst[:, pair, kt * P:(kt + 1) * P],
                                     qst[:, pair, parity, :], start=True, stop=True)
                last.then_inc(qk_done, 1)

            def times_v(i, n):
                g, kt = (n % NU) // NT, n % NT
                at_least(pe, exp_done, 2 * NU * i + 2 * n + 2)
                if n % NU in (0, NU // 2):
                    pe.wait_ge(vaugA_done if n % NU == 0 else vaugB_done, i + 1)
                first, last_of_half = n % (NU // NO) == 0, n % (NU // NO) == NU // NO - 1
                if first:
                    at_least(pe, osb_done, NO * i + g // 2)
                for j in range(NG):
                    last = pe.matmul(oacc[STRIP * j:STRIP * (j + 1), :], vaug[:, kt, NG * g + j, :],
                                     probs[:, kt, j, :], start=first, stop=last_of_half)
                last.then_inc(pv_done, 1)

            def row_max_scores(i):
                for h in range(NH):
                    parity, pair = h % 2, h // 2
                    r = slice(HALF * parity, HALF * parity + PART_ROWS)
                    for t in range(NT):
                        n = NT * h + t
                        at_least(pe, mx_taken, NH * NT * i + n - 3 if n >= 4 else NH * NT * i)
                        pe.matmul(scores[:, n % 4, :], qst[r, pair, parity, t * P:(t + 1) * P], kst[r, pair, :],
                                  start=True, stop=True).then_inc(mx_filled, 1)
                wait_apart(pe, mx_taken, NH * NT * (i + 1), passed)
                pe.transpose(scores[0:NH * NT, 0, 0:P], mx[:, :, :], ident[:, :]).then_inc(mxT_filled, 1)
                pe.wait_ge(shift_loaded, 32 * (i + 1))

            for name in PHASE_PIECES["before"]:
                piece(name, "before", -1)
            prepare_later_weights()
            pe.wait_ge(flag_ready, 1)
            needs_max = pe.value_load(flag[0:1, 0:1], min_val=0, max_val=1)

            def turn(i, phase):
                pe.wait_ge(stackA_loaded, 16 * STACK_DMAS * (i + 1))
                with pe.If(needs_max > 0):
                    pe.wait_ge(stackB_loaded, 16 * STACK_DMAS * (i + 1))
                    at_least(pe, exp_done, 2 * NU * i)
                    row_max_scores(i)
                for u in range(NU):
                    if u == NU // 2:
                        pe.wait_ge(stackB_loaded, 16 * STACK_DMAS * (i + 1))
                    todo = [p for p in SIDE.get(u, []) if p == "b_d1" and phase != "first" or p in PHASE_PIECES[phase]]
                    scores_of(i, u, 0)
                    if u >= 2 or phase != "first":
                        times_v(i, u - 2)
                    scores_of(i, u, 1)
                    for name in todo:
                        piece(name, phase, i)

            turn(0, "first")
            turn(1, "loop")
            with pe.Fori(2, B - 1) as i:
                turn(i, "loop")
            turn(B - 1, "last")
            times_v(B, -2)
            times_v(B, -1)
            for name in PHASE_PIECES["after"]:
                piece(name, "after", B)
                if name == "b_d0":
                    piece("b_d1", "after", B)

        @block.vector
        def _(dve):
            n_prep = [0]

            def prep(ins):
                n_prep[0] += 1
                ins.then_inc(prep_v, 1)
                return n_prep[0]

            def prepare_projections():
                dve.wait_ge(w_loaded, 16 * N_W)
                assert prep(dve.tensor_copy(bv_rep[:, :], bias_col[:, 2:3].broadcast_to((P, P)))) == PREP_REP
                dve.wait_ge(prep_t, 1)
                assert prep(dve.tensor_copy(wrawT[:, :, :],
                                            side[:, 0, 0:3 * D].rearrange("p (k d) -> p k d", k=3))) == PREP_WT
                dve.wait_ge(prep_t, 2)
                prep(dve.tensor_copy(bias_cen[:, :], side[:, 1, 0:2]))
                prep(dve.tensor_copy(bv_row[:, :], side[:, 1, D:2 * D]))
                dve.wait_ge(prep_t, 3)
                assert prep(dve.tensor_copy(wqkv[:, :, :],
                                            side[:, 0, 0:3 * D].rearrange("p (k d) -> p k d", k=3))) == PREP_QKV
                dve.wait_ge(prep_v, PREP_QKV)

            def prepare_small():
                dve.wait_ge(aux_loaded, 16 * N_AUX)
                prep(dve.tensor_scalar(q_aff[:, :], affine[:, 0:2], HD ** -0.5, None, ALU.mult))
                prep(dve.tensor_copy(vb_rep[:, :], affine[:, 5:6].broadcast_to((P, P))))
                prep(dve.tensor_scalar(wo[:, :], wo_raw[:, :], affine[:, 4:5], None, ALU.mult))

            def prepare_int_weights():
                dve.wait_ge(wi_loaded, 48)
                for dst, src, half in ((wg_f, wg_i, 1.0), (wu_f, wu_i, 1.0), (wd_f, wd_i, 0.5)):
                    n = prep(dve.tensor_scalar(dst[:, :, :], src[:, :, :], W_SCALE, half, ALU.mult, ALU.mult))
                assert n == PREP_INT
                dve.wait_ge(prep_v, PREP_INT)
                score_bound()

            def prepare_later_weights():
                for m, wT in enumerate((wgT, wuT, wdT)):
                    dve.wait_ge(prep_t, 4 + m)
                    prep(dve.tensor_copy(wT[:, :, :], side[:, m, 0:NF * P].rearrange("p (j d) -> p j d", j=NF)))
                assert prep(dve.tensor_tensor(out=bo2_row[:, :], in0=side[:, 0, NF * P:NF * P + D],
                                              in1=bo_row[:, :], op=ALU.add)) == PREP_ALL

            def score_bound():
                steps = [0]

                def link(ins):
                    steps[0] += 1
                    ins.then_inc(bound_step, 1)
                    dve.wait_ge(bound_step, steps[0])
                link(dve.tensor_tensor(out=prm2[:, :, :], in0=prm[:, :, :], in1=prm[:, :, :], op=ALU.mult))
                link(dve.reduce_max(bnd[:, 0:2], prm2[:, 0:4:2, :], AX.X))
                link(dve.reduce_sum(bnd[:, 2:4], prm2[:, 1:4:2, :], AX.X))
                link(dve.scalar_tensor_tensor(out=bnd[:, 4:6], in0=bnd[:, 0:2], scalar=float(HD), in1=bnd[:, 2:4],
                                              op0=ALU.mult, op1=ALU.add))
                link(dve.tensor_tensor(out=bnd[:, 6:7], in0=bnd[:, 4:5], in1=bnd[:, 5:6], op=ALU.mult))
                link(dve.tensor_scalar(bnd[:, 7:8], bnd[:, 6:7], SCORE_BOUND ** 2 * HD / 4, -1.0, ALU.is_le, ALU.mult))
                dve.tensor_scalar(flag[:, :], bnd[:, 7:8], 1.0, None, ALU.add).then_inc(flag_ready, 1)

            def norm_stats(b, src, stats, mv, src_ready, stats_done, mv_done):
                src_ready()
                for t in range(NT):
                    dve.bn_stats(stats[:, t, :], src[:, t, :]).then_inc(stats_done, 1)
                for t in range(NT):
                    wait_apart(dve, stats_done, NT * b + t + 1, passed)
                    dve.bn_aggr(mv[:, t, :], stats[:, t, :]).then_inc(mv_done, 1)

            def norm_apply(b, src, dst, mv, rs, rs_done, done):
                dve.wait_ge(rs_done, b + 1)
                for t in range(NT):
                    dve.tensor_scalar(dst[:, t, :], src[:, t, :], mv[:, t, 0:1], rs[:, t:t + 1],
                                      ALU.subtract, ALU.mult).then_inc(done, 1)

            def ln1(b):
                norm_stats(b, x_in, stats1, mv1, lambda: dve.wait_ge(x_loaded, 16 * (b + 1)), stats1_done, mv1_done)
                norm_apply(b, x_in, xn, mv1, rs1, rs1_done, xn_done)

            def copy_xT(b):
                dve.wait_ge(xT_filled, b + 1)
                dve.tensor_copy(xnT[:, :], side[:, BANK["a_xT"], :])\
                   .then_inc(xnT_done, 1)

            def centred(b, w):
                name, sem_f = (("a_q", q_filled), ("a_k", k_filled))[w]
                dve.wait_ge(sem_f, b + 1)
                dve.tensor_scalar(qk_c[:, w, :], side[:, BANK[name], :], bias_cen[:, w:w + 1], None, ALU.add)\
                   .then_inc(qkc_done, 1)

            def centred_v(b):
                dve.wait_ge(v_filled, b + 1)
                at_least(dve, vaugB_done, b)
                dve.tensor_tensor(out=v_c[:, :, :],
                                  in0=side[:, BANK["a_v"], :].rearrange("p (t d) -> p t d", t=NT),
                                  in1=bv_row[:, :].unsqueeze(1).broadcast_to((P, NT, D)), op=ALU.add)\
                   .then_inc(vc_done, 1)

            def variances(b):
                dve.wait_ge(vsq_done, b + 1)
                dve.reduce_sum(v_sum[:, :], v_sq[:, :, :].rearrange("p t (h d) -> p (t h) d", d=HD), AX.X)\
                   .then_inc(vsum_done, 1)
                dve.wait_ge(var_filled, b + 1)
                dve.tensor_scalar(hv[:, 0:2, :, :].rearrange("p w t h -> p (w t h)"),
                                  side[:, BANK["a_var"], 0:2 * NT * NH], HEAD_EPS, None, ALU.add)\
                   .then_inc(hv_done, 1)
                dve.wait_ge(vsum_done, b + 1)
                dve.tensor_scalar(hv[:, 2, :, :].rearrange("p t h -> p (t h)"), v_sum[:, :], 1.0 / HD, HEAD_EPS,
                                  ALU.mult, ALU.add).then_inc(hv_done, 1)
                dve.wait_ge(hv_done, 2 * (b + 1))
                dve.tensor_scalar(hy[:, :, :, :].bitcast(I32), hv[:, :, :, :].bitcast(I32), -0.5, RSQRT_SEED,
                                  ALU.mult, ALU.add).then_inc(seed_done, 1)
                dve.wait_ge(seed_done, b + 1)
                newton_step(b, 0)

            v_all, y_all, t_all = (z[:, :, :, :].rearrange("p w t h -> p (w t h)") for z in (hv, hy, ht))

            def newton_step(b, k):
                def step(ins, n):
                    ins.then_inc(newton, 1)
                    dve.wait_ge(newton, 8 * b + 3 * k + n)
                step(dve.tensor_tensor(out=t_all, in0=y_all, in1=y_all, op=ALU.mult), 1)
                step(dve.scalar_tensor_tensor(out=t_all, in0=t_all, scalar=-0.5, in1=v_all,
                                              op0=ALU.mult, op1=ALU.mult), 2)
                if k < 2:
                    step(dve.scalar_tensor_tensor(out=y_all, in0=t_all, scalar=1.5, in1=y_all,
                                                  op0=ALU.add, op1=ALU.mult), 3)

            def rsqrt_end(b):
                newton_step(b, 1)
                newton_step(b, 2)
                nqk = 2 * NT * NH
                dve.scalar_tensor_tensor(out=hyx[:, :, :, :, :].rearrange("p w t h d -> p (w t h) d"),
                                         in0=t_all[:, 0:nqk].unsqueeze(2).broadcast_to((P, nqk, HD)), scalar=1.5,
                                         in1=y_all[:, 0:nqk].unsqueeze(2).broadcast_to((P, nqk, HD)),
                                         op0=ALU.add, op1=ALU.mult).then_inc(rsqrt_done, 1)
                dve.scalar_tensor_tensor(out=y_all[:, nqk:], in0=t_all[:, nqk:], scalar=1.5, in1=y_all[:, nqk:],
                                         op0=ALU.add, op1=ALU.mult).then_inc(rsqrt_done, 1)

            def normed(b):
                dve.wait_ge(r_filled, 2 * (b + 1))
                for w, name in enumerate(("a_rq", "a_rk")):
                    dve.tensor_tensor(out=qk_n[:, w, :], in0=side[:, BANK[name], :], in1=qk_c[:, w, :], op=ALU.mult)\
                       .then_inc(qkn_done, 1)
                for w in range(2):
                    sc, bi = ((q_aff[:, 0:1], q_aff[:, 1:2]), (affine[:, 2:3], affine[:, 3:4]))[w]
                    dve.wait_ge(qkn_done, 2 * b + w + 1)
                    dve.tensor_scalar(qk_f[:, w, :], qk_n[:, w, :], sc, bi, ALU.mult, ALU.add).then_inc(qkf_done, 1)
                at_least(dve, parts_stored, 16 * PART_DMAS * b)
                dve.wait_ge(qkf_done, 2 * (b + 1))
                dve.tensor_copy(parts[:, 0, :, :], qk_f[:, :, :]).then_inc(part_done, 1)
                dve.wait_ge(part_done, 3 * b + 1)
                dve.tensor_tensor(out=qk_r[:, :, :], in0=qk_f[:, :, :], in1=parts[:, 0, :, :], op=ALU.subtract)\
                   .then_inc(rest_done, 1)

            def lower_parts(b):
                dve.wait_ge(rest_done, b + 1)
                dve.tensor_copy(parts[:, 1, :, :], qk_r[:, :, :]).then_inc(part_done, 1)
                dve.wait_ge(part_done, 3 * b + 2)
                dve.tensor_tensor(out=parts[:, 2, :, :], in0=qk_r[:, :, :], in1=parts[:, 1, :, :], op=ALU.subtract)\
                   .then_inc(part_done, 1)

            def fill_v(b, half):
                at_least(dve, pv_done, NU * b - (NU // 2 if half == 0 else 0))
                if half == 0:
                    dve.wait_ge(rsqrt_done, 2 * (b + 1))
                for k in range(2):
                    hs = slice(NG * (2 * half + k), NG * (2 * half + k + 1))
                    v = v_c[:, :, :].rearrange("p t (h d) -> p t h d", d=HD)[:, :, hs, :]
                    last = dve.tensor_tensor(out=vaug[:, :, hs, HC * k:HC * k + HD], in0=v,
                                             in1=hy[:, 2, :, hs].unsqueeze(3).broadcast_to((P, NT, NG, HD)),
                                             op=ALU.mult)
                last.then_inc(vaugA_done if half == 0 else vaugB_done, 1)

            def divide(b, half):
                o = side[:, BANK[("c_OT0", "b_OT1")[half]], :].rearrange("p (t j x) -> p t j x", t=NT, j=NG)
                dve.wait_ge(OT_filled, NO * b + half + 1)
                if half == 0:
                    at_least(dve, onT_filled, b)
                at_least(dve, on_done, NO * b + half)
                for k in range(2):
                    last = dve.reciprocal(rinv[:, k, :, :], o[:, :, :, HC * k + HD])
                last.then_inc(rinv_done, 1)
                dve.wait_ge(rinv_done, NO * b + half + 1)
                for k in range(2):
                    h0 = NG * (2 * half + k)
                    last = dve.tensor_tensor(
                        out=on[:, :, h0 * HD:(h0 + NG) * HD].rearrange("p t (j d) -> p t j d", d=HD),
                        in0=o[:, :, :, HC * k:HC * k + HD],
                        in1=rinv[:, k, :, :].unsqueeze(3).broadcast_to((P, NT, NG, HD)), op=ALU.mult)
                last.then_inc(on_done, 1)

            def copy_onT(b):
                dve.wait_ge(onT_filled, b + 1)
                dve.tensor_copy(onT[:, :], side[:, BANK["b_onT"], :])\
                   .then_inc(onT_done, 1)

            def ln2_stats(b):
                dve.wait_ge(Wo_filled, b + 1)
                dve.wait_ge(xbo_done, b + 1)
                dve.tensor_tensor(out=x2[:, :, :], in0=side[:, BANK["b_Wo"], :].rearrange("p (t d) -> p t d", t=NT),
                                  in1=x_bo[:, :, :], op=ALU.add).then_inc(x2_done, 1)
                norm_stats(b, x2, stats2, mv2, lambda: dve.wait_ge(x2_done, b + 1), stats2_done, mv2_done)

            def ln2_apply(b):
                norm_apply(b, x2, x2n, mv2, rs2, rs2_done, x2n_done)

            def copy_x2T(b):
                dve.wait_ge(x2T_filled, b + 1)
                dve.tensor_copy(x2T[:, :], side[:, BANK["b_x2T"], :])\
                   .then_inc(x2T_done, 1)

            def silu_up(b, j):
                dve.wait_ge(tanh_done, NF * b + j + 1)
                dve.scalar_tensor_tensor(out=ga[:, j, :], in0=th[:, j, :], scalar=1.0, in1=side[:, BANK[f"b_g{j}"], :],
                                         op0=ALU.add, op1=ALU.mult)\
                   .then_inc(ga_done, 1)
                dve.wait_ge(u_filled, NF * b + j + 1)
                dve.wait_ge(ga_done, NF * b + j + 1)
                dve.tensor_tensor(out=hT[:, j, :], in0=side[:, BANK[f"b_u{j}"], :], in1=ga[:, j, :], op=ALU.mult)\
                   .then_inc(h_done, 1)

            def result(b):
                dve.wait_ge(d_filled, b + 1)
                at_least(dve, out_stored, 16 * b)
                dve.tensor_tensor(out=y[:, :, :], in0=side[:, BANK["b_d0"], :].rearrange("p (t d) -> p t d", t=NT),
                                  in1=x2[:, :, :], op=ALU.add).then_inc(y_done, 1)

            def row_maxima(i):
                for n in range(NH * NT):
                    dve.wait_ge(mx_filled, NH * NT * i + n + 1)
                    dve.tensor_reduce(out=mx[:, n // NT, n % NT:n % NT + 1], in_=scores[:, n % 4, :], axis=AX.X,
                                      op=ALU.max, negate=True).then_inc(mx_taken, 1)
                dve.wait_ge(mxT_filled, i + 1)
                at_least(dve, maxes_stored, 32 * i)
                dve.tensor_copy(mx_hi[:, :], scores[0:NH * NT, 0, 0:P]).then_inc(mx_parts, 1)
                dve.wait_ge(mx_parts, 2 * i + 1)
                dve.tensor_tensor(out=mx_lo[:, :], in0=scores[0:NH * NT, 0, 0:P], in1=mx_hi[:, :], op=ALU.subtract)\
                   .then_inc(mx_parts, 1)

            ln1(0)
            prepare_projections()
            copy_xT(0)
            centred(0, 0)
            centred(0, 1)
            centred_v(0)
            prepare_small()
            variances(0)
            rsqrt_end(0)
            normed(0)
            lower_parts(0)
            dve.wait_ge(consts, 3)
            prepare_int_weights()
            fill_v(0, 0)
            prepare_later_weights()
            dve.wait_ge(flag_ready, 1)
            needs_max = dve.value_load(flag[0:1, 0:1], min_val=0, max_val=1)

            def turn(i, phase):
                ahead = phase in ("first", "loop")
                behind = phase != "first"
                with dve.If(needs_max > 0):
                    row_maxima(i)
                if ahead:
                    ln1(i + 1)
                    copy_xT(i + 1)
                fill_v(i, 1)
                if behind:
                    divide(i - 1, 1)
                if ahead:
                    centred(i + 1, 0)
                if behind:
                    copy_onT(i - 1)
                if ahead:
                    centred(i + 1, 1)
                if behind:
                    ln2_stats(i - 1)
                if ahead:
                    centred_v(i + 1)
                if behind:
                    ln2_apply(i - 1)
                if ahead:
                    variances(i + 1)
                if behind:
                    copy_x2T(i - 1)
                if ahead:
                    rsqrt_end(i + 1)
                    normed(i + 1)
                if behind:
                    silu_up(i - 1, 0)
                if ahead:
                    lower_parts(i + 1)
                if behind:
                    silu_up(i - 1, 1)
                divide(i, 0)
                if ahead:
                    fill_v(i + 1, 0)
                if behind:
                    silu_up(i - 1, 2)
                    result(i - 1)

            turn(0, "first")
            turn(1, "loop")
            with dve.Fori(2, B - 1) as i:
                turn(i, "loop")
            turn(B - 1, "last")
            divide(B - 1, 1)
            copy_onT(B - 1)
            ln2_stats(B - 1)
            ln2_apply(B - 1)
            copy_x2T(B - 1)
            for j in range(NF):
                silu_up(B - 1, j)
            result(B - 1)


INPUTS = ["L0_attn_x", "L0_attn_Wq", "L0_attn_bq", "L0_attn_Wk", "L0_attn_bk", "L0_attn_Wv", "L0_attn_bv",
          "L0_attn_q_scale", "L0_attn_q_bias", "L0_attn_k_scale", "L0_attn_k_bias", "L0_attn_v_scale",
          "L0_attn_v_bias", "L0_attn_Wo", "L0_attn_bo", "L0_ffn_w_gate", "L0_ffn_w_up", "L0_ffn_w_down"]


def kernel(**inputs):
    from concourse import bacc
    from concourse.bass_utils import run_bass_kernel_spmd

    nc = bacc.Bacc("TRN2", target_bir_lowering=False, num_devices=1)
    arrays, args = {}, []
    for name in INPUTS:
        a = np.ascontiguousarray(inputs[name])
        arrays["in_" + name] = a
        args.append(nc.dram_tensor("in_" + name, a.shape, mybir.dt.from_np(a.dtype), kind="ExternalInput").ap())
    parts = nc.dram_tensor("parts_dram", (2, P, 6, S), BF16, kind="Internal").ap()
    maxes = nc.dram_tensor("maxes_dram", (2, NH, NT, P), BF16, kind="Internal").ap()
    out = nc.dram_tensor("out_dram", (B, S, D), F32, kind="ExternalOutput").ap()
    build(nc, *args, parts, maxes, out)
    r = run_bass_kernel_spmd(nc, [arrays], core_ids=[0])
    return r.results[0]["out_dram"]
```

```python
import numpy as np
import concourse.bass as bass
from concourse import mybir
from contextlib import ExitStack

F32 = mybir.dt.float32
BF16 = mybir.dt.bfloat16
I32 = mybir.dt.int32
ALU = mybir.AluOpType
ACT = mybir.ActivationFunctionType
AX = mybir.AxisListType

B, S, D = 8, 512, 128
NH, HD = 16, 8
HID = 384
P = 128
NT = S // P
NF = HID // P
NG = 4
NU = NG * NT
PAIRS = NH // 2
STRIP = 32
HC = HD + 1
NO = 2
PART_ROWS = 6 * HD
SHIFT_ROWS = 2
ROWS = PART_ROWS + SHIFT_ROWS
HALF = 64
LN_EPS, HEAD_EPS = 1e-5, 1e-6
W_SCALE = float(np.float32(1.0 / 127.0))
SCORE_BOUND = 60.0
RSQRT_SEED = float(0x5F3759DF)
PLACES = [[(0, 0, 1, 3), (1, 0, 3, 2), (1, 5, 1, 1)], [(0, 3, 1, 2), (1, 1, 3, 2)], [(0, 5, 1, 1), (1, 2, 1, 1)]]
WARM_UP = 10
STACK_DMAS = 2 * 2
PART_DMAS = sum(len(p) for p in PLACES)

SIDE = {1: ["a_xT"], 2: ["b_OT1", "a_q"], 3: ["b_onT", "a_k"], 4: ["b_Wo", "a_v"], 5: ["a_var"],
        6: ["b_x2T"], 7: ["b_g0"], 8: ["a_rq", "a_rk"], 9: ["b_u0", "b_g1"], 10: ["b_u1", "c_OT0"],
        11: ["b_g2", "b_u2"], 13: ["b_d0"], 14: ["b_d1"]}
BANK = {"a_xT": 0, "b_OT1": 1, "a_q": 2, "b_onT": 0, "a_k": 1, "b_Wo": 2, "a_v": 0, "a_var": 1,
        "b_x2T": 2, "b_g0": 0, "a_rq": 1, "a_rk": 2, "b_u0": 1, "b_g1": 2, "b_u1": 0, "c_OT0": 1, "b_g2": 2,
        "b_u2": 0, "b_d0": 1}
LAST_SLOTS = {6: [], 7: ["b_x2T"], 8: ["b_g0"]}
SIDE_ORDER = [p for u in range(NU) for p in SIDE.get(u, []) if p != "b_d1"]
PHASE_PIECES = {
    "before": ["a_xT", "a_v", "a_q", "a_k", "a_var", "a_rq", "a_rk"],
    "first": [p for p in SIDE_ORDER if p[0] != "b"],
    "loop": SIDE_ORDER,
    "last": [p for p in SIDE_ORDER if p[0] != "a"],
}

EARLY = ["a_xT", "a_q", "a_k", "a_v", "a_var"]


def sequence_of(piece, i):
    return {"a": i + 1, "b": i - 1, "c": i}[piece[0]]


def occupants_before(phase, i, piece):
    def same_bank(p):
        return BANK[p] == BANK[piece]
    own = [p for p in PHASE_PIECES[phase] if same_bank(p)]
    k = own.index(piece)
    if k:
        return [(own[k - 1], sequence_of(own[k - 1], i))]
    before = {"before": [], "first": ["before"], "loop": ["first", "loop"], "last": ["loop"]}
    lasts = {[p for p in PHASE_PIECES[ph] if same_bank(p)][-1] for ph in before[phase]}
    return [(p, sequence_of(p, i - 1)) for p in sorted(lasts)]


def at_least(eng, sem, value):
    if not (isinstance(value, int) and value <= 0):
        eng.wait_ge(sem, value)


def wait_apart(eng, sem, value, passed):
    at_least(eng, sem, value)
    eng.sem_inc(passed, 1)


def build(nc, x_d, Wq_d, bq_d, Wk_d, bk_d, Wv_d, bv_d, qs_d, qb_d, ks_d, kb_d, vs_d, vb_d, Wo_d, bo_d,
          wg_d, wu_d, wd_d, parts_d, maxes_d, out_d):
    ctx = ExitStack()
    with ctx:
        def sb(name, shape, dt=F32):
            return ctx.enter_context(nc.sbuf_tensor(name, shape, dt))

        def ps(name, shape, dt=F32):
            return ctx.enter_context(nc.psum_tensor(name, shape, dt))

        def sem(name):
            return ctx.enter_context(nc.semaphore(name))

        ident = sb("ident", [P, P])
        group8 = sb("group8", [P, P])
        center = sb("center", [P, P])
        wraw = sb("wraw", [P, 4, D])
        head_sum = sb("head_sum", [P, 4 * NH])
        wqkv = sb("wqkv", [P, 4, D])
        bias_col = sb("bias_col", [P, 2])
        bias_cen = sb("bias_cen", [P, 2])
        affine = sb("affine", [P, 6])
        q_aff = sb("q_aff", [P, 2])
        vb_rep = sb("vb_rep", [P, P])
        wo_raw = sb("wo_raw", [P, D])
        wo = sb("wo", [P, D])
        bo_row = sb("bo_row", [P, D])
        bo2_row = sb("bo2_row", [P, D])
        wg_i = sb("wg_i", [P, NF, D], I32)
        wu_i = sb("wu_i", [P, NF, D], I32)
        wd_i = sb("wd_i", [P, NF, D], I32)
        wg_f = sb("wg_f", [P, NF, D])
        wu_f = sb("wu_f", [P, NF, D])
        wd_f = sb("wd_f", [P, NF, D])
        wgT = sb("wgT", [P, NF, P])
        wuT = sb("wuT", [P, NF, P])
        wdT = sb("wdT", [P, NF, P])
        neg_half = sb("neg_half", [P, NT])
        prm = sb("prm", [1, 4, HD])
        prm2 = sb("prm2", [1, 4, HD])
        bnd = sb("bnd", [1, 8])
        flag = sb("flag", [1, 1], I32)

        x_in = sb("x_in", [P, NT, D])
        stats1 = sb("stats1", [P, NT, 6])
        mv1 = sb("mv1", [P, NT, 2])
        ve1 = sb("ve1", [P, NT])
        rs1 = sb("rs1", [P, NT])
        xn = sb("xn", [P, NT, D])
        xnT = sb("xnT", [P, S])
        qk_c = sb("qk_c", [P, 2, S])
        qk_sq = sb("qk_sq", [P, 2, S])
        v_c = sb("v_c", [P, NT, D])
        v_sq = sb("v_sq", [P, NT, D])
        v_sum = sb("v_sum", [P, NT * NH])
        hv = sb("hv", [P, 3, NT, NH])
        hy = sb("hy", [P, 3, NT, NH])
        ht = sb("ht", [P, 3, NT, NH])
        hyx = sb("hyx", [P, 2, NT, NH, HD])
        qk_n = sb("qk_n", [P, 2, S])
        qk_f = sb("qk_f", [P, 2, S])
        qk_r = sb("qk_r", [P, 2, S])
        parts = sb("parts", [P, 3, 2, S], BF16)
        qst = sb("qst", [P, PAIRS, 2, S], BF16)
        kst = sb("kst", [P, PAIRS, S], BF16)
        vaug = sb("vaug", [P, NT, NH, STRIP])
        probs = sb("probs", [P, NT, NG, S])
        osb = sb("osb", [P, S])
        rinv = sb("rinv", [P, 2, NT, NG])
        on = sb("on", [P, NT, D])
        mx = sb("mx", [P, NH, NT])
        mx_hi = sb("mx_hi", [NH * NT, P], BF16)
        mx_lo = sb("mx_lo", [NH * NT, P], BF16)
        x_res = sb("x_res", [P, NT, D])
        x_bo = sb("x_bo", [P, NT, D])
        onT = sb("onT", [P, S])
        x2 = sb("x2", [P, NT, D])
        stats2 = sb("stats2", [P, NT, 6])
        mv2 = sb("mv2", [P, NT, 2])
        ve2 = sb("ve2", [P, NT])
        rs2 = sb("rs2", [P, NT])
        x2n = sb("x2n", [P, NT, D])
        x2T = sb("x2T", [P, S])
        th = sb("th", [P, NF, S])
        ga = sb("ga", [P, NF, S])
        hT = sb("hT", [P, NF, S])
        y = sb("y", [P, NT, D])

        scores = ps("scores", [P, 4, S])
        oacc = ps("oacc", [P, S])
        side = ps("side", [P, 3, S])

        w_loaded = sem("w_loaded")
        bias_loaded = sem("bias_loaded")
        prm_loaded = sem("prm_loaded")
        wi_loaded = sem("wi_loaded")
        aux_loaded = sem("aux_loaded")
        x_loaded = sem("x_loaded")
        xres_loaded = sem("xres_loaded")
        parts_stored = sem("parts_stored")
        stackA_loaded = sem("stackA_loaded")
        stackB_loaded = sem("stackB_loaded")
        out_stored = sem("out_stored")
        maxes_stored = sem("maxes_stored")
        shift_loaded = sem("shift_loaded")
        passed = sem("passed")
        filled = sem("filled")
        consts = sem("consts")
        head_sums_done = sem("head_sums_done")
        w_centred = sem("w_centred")
        bias_filled = sem("bias_filled")
        bias_centred = sem("bias_centred")
        small_done = sem("small_done")
        ints_floated = sem("ints_floated")
        bo2_filled = sem("bo2_filled")
        bo2_done = sem("bo2_done")
        wT_filled = sem("wT_filled")
        wT_copied = sem("wT_copied")
        bound_step = sem("bound_step")
        flag_ready = sem("flag_ready")
        stacks_init = sem("stacks_init")
        stats1_done = sem("stats1_done")
        mv1_done = sem("mv1_done")
        ve1_done = sem("ve1_done")
        rs1_done = sem("rs1_done")
        xn_done = sem("xn_done")
        xT_filled = sem("xT_filled")
        xnT_done = sem("xnT_done")
        q_filled = sem("q_filled")
        k_filled = sem("k_filled")
        v_filled = sem("v_filled")
        qkc_done = sem("qkc_done")
        vc_done = sem("vc_done")
        vsq_done = sem("vsq_done")
        vsum_done = sem("vsum_done")
        qksq_done = sem("qksq_done")
        var_filled = sem("var_filled")
        hv_done = sem("hv_done")
        seed_done = sem("seed_done")
        newton = sem("newton")
        rsqrt_done = sem("rsqrt_done")
        r_filled = sem("r_filled")
        qkn_done = sem("qkn_done")
        qkf_done = sem("qkf_done")
        part_done = sem("part_done")
        rest_done = sem("rest_done")
        vaugA_done = sem("vaugA_done")
        vaugB_done = sem("vaugB_done")
        qk_done = sem("qk_done")
        exp_done = sem("exp_done")
        pv_done = sem("pv_done")
        osb_done = sem("osb_done")
        OT_filled = sem("OT_filled")
        rinv_done = sem("rinv_done")
        on_done = sem("on_done")
        mx_filled = sem("mx_filled")
        mx_taken = sem("mx_taken")
        mxT_filled = sem("mxT_filled")
        mx_parts = sem("mx_parts")
        onT_filled = sem("onT_filled")
        onT_done = sem("onT_done")
        xbo_done = sem("xbo_done")
        Wo_filled = sem("Wo_filled")
        x2_done = sem("x2_done")
        stats2_done = sem("stats2_done")
        mv2_done = sem("mv2_done")
        ve2_done = sem("ve2_done")
        rs2_done = sem("rs2_done")
        x2n_done = sem("x2n_done")
        x2T_filled = sem("x2T_filled")
        x2T_done = sem("x2T_done")
        g_filled = sem("g_filled")
        u_filled = sem("u_filled")
        tanh_done = sem("tanh_done")
        ga_done = sem("ga_done")
        h_done = sem("h_done")
        d_filled = sem("d_filled")
        y_done = sem("y_done")
        read_out = {"xT": (xnT_done, 1, 0), "q": (qkc_done, 2, 0), "k": (qkc_done, 2, 1), "v": (vc_done, 1, 0),
                    "var": (hv_done, 2, 0), "rq": (qkn_done, 2, 0), "rk": (qkn_done, 2, 1),
                    "onT": (onT_done, 1, 0), "Wo": (x2_done, 1, 0), "x2T": (x2T_done, 1, 0), "d0": (y_done, 1, 0)}
        read_out.update({f"OT{o}": (on_done, NO, o) for o in range(NO)})
        read_out.update({f"g{j}": (ga_done, NF, j) for j in range(NF)})
        read_out.update({f"u{j}": (h_done, NF, j) for j in range(NF)})

        x_t = x_d.rearrange("b (p t) d -> b p t d", t=NT)
        out_t = out_d.rearrange("b (p t) d -> b p t d", t=NT)
        head_vec = [qs_d, qb_d, ks_d, kb_d, vs_d, vb_d]
        N_W, N_AUX = 3 + 1, 6 + 2

        OTs = [side[:, 1, :], side[:, 0, :]]
        onTs = [scores[:, 1, :], scores[:, 2, :]]
        Wos = [scores[:, 0, :], scores[:, 3, :]]
        x2Ts = [side[:, 2, :], oacc[:, :]]
        last_gates = [scores[:, j, :] for j in range(NF)]
        last_ups = [scores[:, 3, :], side[:, 0, :], side[:, 1, :]]
        last_downs = [oacc[:, 0:D], side[:, 2, 0:D], scores[:, 0, 0:D], scores[:, 1, 0:D]]
        HALF_TILES = NT // 2
        half_cols = [slice(0, S // 2), slice(S // 2, S)]
        half_tiles = [range(0, HALF_TILES), range(HALF_TILES, NT)]

        block = ctx.enter_context(nc.Block())

        @block.sync
        def _(sp):
            def load_x(b):
                if not (isinstance(b, int) and b == 0):
                    wait_apart(sp, xn_done, NT * b, passed)
                sp.dma_start(x_in[:, :, :], x_t[b, :, :, :]).then_inc(x_loaded, 16)

            def store_parts(b):
                if not (isinstance(b, int) and b == 0):
                    wait_apart(sp, stackB_loaded, 16 * STACK_DMAS * b, passed)
                for part, places in enumerate(PLACES):
                    wait_apart(sp, part_done, 3 * b + part + 1, passed)
                    for which, slot, step, n in places:
                        src = parts[:, part:part + 1, which, :]
                        sp.dma_start(parts_d[which, :, slot:slot + step * (n - 1) + 1:step, :],
                                     src if n == 1 else src.broadcast_to((P, n, S))).then_inc(parts_stored, 16)

            def load_stack(b, half, loaded):
                wait_apart(sp, parts_stored, 16 * PART_DMAS * (b + 1), passed)
                if not (isinstance(b, int) and b == 0):
                    wait_apart(sp, qk_done, 2 * NU * b - (NU if half == 0 else 0), passed)
                for parity in range(2):
                    for which, stack in ((0, qst[:, :, parity, :]), (1, kst[:, :, :])):
                        r0 = HALF * parity
                        src = parts_d[which].rearrange("(c z d) r s -> z (d r) c s", z=2, d=HD)[parity]
                        sp.dma_start(stack[r0:r0 + PART_ROWS, 4 * half:4 * half + 4, :],
                                     src[:, 4 * half:4 * half + 4, :]).then_inc(loaded, 16)

            def load_res(b):
                wait_apart(sp, xbo_done, b, passed)
                sp.dma_start(x_res[:, :, :], x_t[b, :, :, :]).then_inc(xres_loaded, 16)

            def store_out(b):
                wait_apart(sp, y_done, b + 1, passed)
                sp.dma_start(out_t[b, :, :, :], y[:, :, :]).then_inc(out_stored, 16)

            def shift_rows(i):
                sp.wait_ge(mx_parts, 2 * (i + 1))
                for part, src in enumerate((mx_hi, mx_lo)):
                    sp.dma_start(maxes_d[part].rearrange("h t p -> (h t) p"), src[:, :])\
                      .then_inc(maxes_stored, 16)
                sp.wait_ge(maxes_stored, 32 * (i + 1))
                for parity in range(2):
                    r0 = HALF * parity + PART_ROWS
                    sp.dma_start(qst[r0:r0 + 2, :, parity, :],
                                 maxes_d.rearrange("r (c z) t p -> z r c (t p)", z=2)[parity])\
                      .then_inc(shift_loaded, 16)

            load_x(0)
            sp.wait_ge(w_loaded, 16 * N_W)
            for dst, src in ((wg_i, wg_d.rearrange("(j p) d -> p j d", p=P)),
                             (wu_i, wu_d.rearrange("(j p) d -> p j d", p=P)),
                             (wd_i, wd_d.rearrange("p (j h) -> p j h", j=NF))):
                sp.dma_start(dst[:, :, :], src).then_inc(wi_loaded, 16)
            load_x(1)
            for k, src in enumerate(head_vec[:4]):
                sp.dma_start(prm[:, k, :], src.rearrange("(a n) -> a n", a=1)).then_inc(prm_loaded, 16)
            for k, src in enumerate(head_vec):
                sp.dma_start(affine[:, k:k + 1],
                             src.rearrange("(a d b) -> a d b", a=1, b=1).broadcast_to((NH, HD, 1)))\
                  .then_inc(aux_loaded, 16)
            sp.dma_start(wo_raw[:, :], Wo_d).then_inc(aux_loaded, 16)
            sp.dma_start(bo_row[:, :], bo_d.rearrange("(a n) -> a n", a=1).broadcast_to((P, D)))\
              .then_inc(aux_loaded, 16)
            load_res(0)
            sp.wait_ge(stacks_init, 2)
            store_parts(0)
            load_stack(0, 0, stackA_loaded)
            sp.wait_ge(flag_ready, 1)
            needs_max = sp.value_load(flag[0:1, 0:1], min_val=0, max_val=1)

            def turn(i, phase):
                load_stack(i, 1, stackB_loaded)
                with sp.If(needs_max > 0):
                    shift_rows(i)
                if not (isinstance(i, int) and i + 2 >= B):
                    load_x(i + 2)
                if phase in ("first", "loop"):
                    store_parts(i + 1)
                    load_stack(i + 1, 0, stackA_loaded)
                if phase in ("loop", "last"):
                    load_res(i)
                    store_out(i - 1)

            turn(0, "first")
            turn(1, "loop")
            with sp.Fori(2, B - 2) as i:
                turn(i, "loop")
            turn(B - 2, "loop")
            turn(B - 1, "last")
            store_out(B - 1)
            sp.wait_ge(out_stored, 16 * B)
            sp.wait_ge(parts_stored, 16 * PART_DMAS * B)
            with sp.If(needs_max > 0):
                sp.wait_ge(maxes_stored, 32 * B)

        @block.gpsimd
        def _(pool):
            pool.memset(ident[:, :], 0.0).then_inc(filled, 1)
            pool.memset(group8[:, :], 1.0 / HD).then_inc(filled, 1)
            pool.memset(neg_half[:, :], -0.5).then_inc(filled, 1)
            pool.wait_ge(filled, 3)
            pool.affine_select(out=ident[:, :], in_=ident[:, :], compare_op=ALU.not_equal, fill=1.0, base=0,
                               pattern=[[-1, P]], channel_multiplier=1).then_inc(filled, 1)
            blocks = group8[:, :].rearrange("p (h d) -> p h d", d=HD)
            pool.affine_select(out=blocks, in_=blocks, compare_op=ALU.is_ge, fill=0.0, base=0,
                               pattern=[[-HD, NH], [0, HD]], channel_multiplier=1).then_inc(filled, 1)
            pool.wait_ge(filled, 5)
            pool.affine_select(out=blocks, in_=blocks, compare_op=ALU.is_ge, fill=0.0, base=HD - 1,
                               pattern=[[HD, NH], [0, HD]], channel_multiplier=-1).then_inc(filled, 1)
            pool.wait_ge(filled, 6)
            pool.tensor_tensor(out=center[:, :], in0=ident[:, :], in1=group8[:, :], op=ALU.subtract)\
                .then_inc(consts, 1)
            def norm_power(b, mv, ve, rs, mv_done, ve_done, rs_done, half=None):
                tiles, n = (range(NT), 0) if half is None else (half_tiles[half], half)
                ts = slice(tiles[0], tiles[-1] + 1)
                wait_apart(pool, mv_done, NT * b + tiles[-1] + 1, passed)
                pool.tensor_scalar(ve[:, ts], mv[:, ts, 1], LN_EPS, None, ALU.add).then_inc(ve_done, 1)
                pool.wait_ge(ve_done, b + 1 + n)
                pool.tensor_tensor(out=rs[:, ts], in0=ve[:, ts], in1=neg_half[:, ts], op=ALU.pow).then_inc(rs_done, 1)

            def v_squares(b):
                pool.wait_ge(vc_done, b + 1)
                pool.tensor_tensor(out=v_sq[:, :, :], in0=v_c[:, :, :], in1=v_c[:, :, :], op=ALU.mult)\
                    .then_inc(vsq_done, 1)

            def residual(b):
                pool.wait_ge(xres_loaded, 16 * (b + 1))
                at_least(pool, x2_done, b)
                pool.tensor_tensor(out=x_bo[:, :, :], in0=x_res[:, :, :],
                                   in1=bo2_row[:, :].unsqueeze(1).broadcast_to((P, NT, D)), op=ALU.add)\
                    .then_inc(xbo_done, 1)

            norm_power(0, mv1, ve1, rs1, mv1_done, ve1_done, rs1_done)
            pool.memset(vaug[:, :, :, :], 0.0).then_inc(filled, 1)
            pool.wait_ge(filled, 7)
            for k in range(2):
                ones = vaug[:, :, :, HC * k + HD].rearrange("p t (o k j) -> p k (t o) j", k=2, j=NG)[:, k, :, :]
                pool.memset(ones, 1.0).then_inc(consts, 1)

            pool.memset(qst[:, :, :, :].bitcast(I32), 0).then_inc(stacks_init, 1)
            norm_power(1, mv1, ve1, rs1, mv1_done, ve1_done, rs1_done)
            pool.memset(kst[:, :, :], 1.0).then_inc(stacks_init, 1)
            v_squares(1)
            pool.wait_ge(bo2_done, 1)

            def turn(i, phase):
                if phase == "loop":
                    norm_power(i + 1, mv1, ve1, rs1, mv1_done, ve1_done, rs1_done)
                residual(i - 1)
                norm_power(i - 1, mv2, ve2, rs2, mv2_done, ve2_done, rs2_done)
                if phase == "loop":
                    v_squares(i + 1)

            turn(1, "loop")
            with pool.Fori(2, B - 1) as i:
                turn(i, "loop")
            turn(B - 1, "last")
            residual(B - 1)
            for half in range(2):
                norm_power(B - 1, mv2, ve2, rs2, mv2_done, ve2_done, rs2_done, half)

        @block.scalar
        def _(act):
            for k, src in enumerate((Wq_d, Wk_d, Wv_d)):
                act.dma_start(wraw[:, k, :], src).then_inc(w_loaded, 16)
            act.dma_start(wraw[:, 3, :], bv_d.rearrange("(a n) -> a n", a=1).broadcast_to((P, D)))\
               .then_inc(w_loaded, 16)
            for k, src in enumerate((bq_d, bk_d)):
                act.dma_start(bias_col[:, k:k + 1], src.rearrange("(p a) -> p a", a=1)).then_inc(bias_loaded, 16)
            act.wait_ge(wi_loaded, 48)
            for dst, src, factor in ((wg_f, wg_i, W_SCALE), (wu_f, wu_i, W_SCALE), (wd_f, wd_i, W_SCALE / 2)):
                act.activation(dst[:, :, :], src[:, :, :], ACT.Copy, scale=factor).then_inc(ints_floated, 1)

            def tanh(b, j, gate):
                act.wait_ge(g_filled, NF * b + j + 1)
                act.activation(th[:, j, :], gate, ACT.Tanh, scale=0.5).then_inc(tanh_done, 1)

            def copy_o(b, o):
                act.wait_ge(pv_done, NU * b + NU // NO * (o + 1))
                at_least(act, OT_filled, NO * b + o)
                act.activation(osb[:, :], oacc[:, :], ACT.Copy).then_inc(osb_done, 1)

            def squares(b):
                for w in range(2):
                    act.wait_ge(qkc_done, 2 * b + w + 1)
                    act.activation(qk_sq[:, w, :], qk_c[:, w, :], ACT.Square).then_inc(qksq_done, 1)

            act.wait_ge(vc_done, 1)
            act.activation(v_sq[:, :, :], v_c[:, :, :], ACT.Square).then_inc(vsq_done, 1)
            squares(0)
            for m, wT in enumerate((wgT, wuT, wdT)):
                act.wait_ge(wT_filled, m + 1)
                act.activation(wT[:, :, :], scores[:, m, 0:NF * P].rearrange("p (j d) -> p j d", j=NF), ACT.Copy)\
                   .then_inc(wT_copied, 1)
            act.wait_ge(xT_filled, 2)
            act.activation(xnT[:, :], side[:, BANK["a_xT"], :], ACT.Copy).then_inc(xnT_done, 1)
            squares(1)
            SQUARES_AT = 4
            TANH_AT = {"loop": {7: 0, 9: 1, 11: 2}, "last": {8: 0, 9: 1, 11: 2}}

            def turn(i, phase):
                for u in range(NU):
                    kt = u % NT
                    at_least(act, pv_done, NU * i + u - NT + 1)
                    for c in range(2):
                        act.wait_ge(qk_done, 2 * NU * i + 2 * u + c + 1)
                        act.activation(probs[:, kt, 2 * c:2 * c + 2, :], scores[:, 2 * c:2 * c + 2, :], ACT.Exp)\
                           .then_inc(exp_done, 1)
                        if c == 0 and u == 1 and phase != "first":
                            copy_o(i - 1, 1)
                        if c == 0 and u == NU // NO + 1:
                            copy_o(i, 0)
                    if phase == "loop" and u == SQUARES_AT:
                        squares(i + 1)
                    if phase != "first" and u in TANH_AT[phase]:
                        j = TANH_AT[phase][u]
                        tanh(i - 1, j, side[:, BANK[f"b_g{j}"], :])

            turn(0, "first")
            turn(1, "loop")
            with act.Fori(2, B - 1) as i:
                turn(i, "loop")
            turn(B - 1, "last")
            act.wait_ge(pv_done, NU * B)
            act.wait_ge(OT_filled, NO * (B - 1) + 1)
            for cols in half_cols:
                act.activation(osb[:, cols], oacc[:, cols], ACT.Copy).then_inc(osb_done, 1)
            for j in range(NF):
                tanh(B - 1, j, last_gates[j])

        @block.tensor
        def _(pe):
            pe.wait_ge(filled, 4)
            for _ in range(WARM_UP):
                pe.matmul(scores[:, 3, 0:P], ident[:, :], ident[:, :], start=True, stop=True)
            pe.wait_ge(consts, 1)
            pe.wait_ge(bias_loaded, 32)
            for k in range(2):
                last = pe.matmul(scores[:, 0, k:k + 1], center[:, :], bias_col[:, k:k + 1], start=True, stop=True)
            last.then_inc(bias_filled, 1)

            def prepare_later_weights():
                pe.wait_ge(bias_centred, 1)
                for m, w in enumerate((wg_f, wu_f, wd_f)):
                    pe.wait_ge(ints_floated, m + 1)
                    for j in range(NF):
                        last = pe.transpose(scores[:, m, j * P:(j + 1) * P], w[:, j, :], ident[:, :])
                    last.then_inc(wT_filled, 1)
                pe.wait_ge(small_done, 3)
                pe.matmul(scores[:, 3, 0:D], vb_rep[:, :], wo_raw[:, :], start=True, stop=True).then_inc(bo2_filled, 1)

            def bank_free(phase, i, piece):
                for p, b in occupants_before(phase, i, piece):
                    done, per_sequence, place = read_out[p[2:]]
                    at_least(pe, done, per_sequence * b + place + 1)
                return side[:, BANK[piece], :]

            def transposes(dst, src, tiles=range(NT)):
                for k, t in enumerate(tiles):
                    last = pe.transpose(dst[:, k * P:(k + 1) * P], src(t), ident[:, :])
                return last

            def piece(name, phase, i):
                what = name[2:]
                b = sequence_of(name, i)
                if name != "b_d1":
                    bank = bank_free(phase, i, name)
                else:
                    bank = side[:, BANK["b_d0"], :]
                if what == "xT":
                    pe.wait_ge(xn_done, NT * (b + 1))
                    transposes(bank, lambda t: xn[:, t, :]).then_inc(xT_filled, 1)
                elif what in ("q", "k"):
                    pe.wait_ge(xnT_done, b + 1)
                    w = 0 if what == "q" else 1
                    pe.matmul(bank, wqkv[:, w, :], xnT[:, :], start=True, stop=True)\
                      .then_inc(q_filled if what == "q" else k_filled, 1)
                elif what == "v":
                    pe.wait_ge(xnT_done, b + 1)
                    for t in range(NT):
                        last = pe.matmul(bank[:, t * D:(t + 1) * D], xnT[:, t * P:(t + 1) * P], wqkv[:, 2, :],
                                         start=True, stop=True)
                    last.then_inc(v_filled, 1)
                elif what == "var":
                    for w in range(2):
                        pe.wait_ge(qksq_done, 2 * b + w + 1)
                        for t in range(NT):
                            o = (w * NT + t) * NH
                            last = pe.matmul(bank[:, o:o + NH], qk_sq[:, w, t * P:(t + 1) * P],
                                             group8[:, 0:P:HD], start=True, stop=True)
                    last.then_inc(var_filled, 1)
                elif what in ("rq", "rk"):
                    w = 0 if what == "rq" else 1
                    pe.wait_ge(rsqrt_done, 3 * b + w + 1)
                    transposes(bank, lambda t: hyx[:, w, t, :, :])\
                        .then_inc(r_filled, 1)
                elif what[:2] == "OT":
                    pe.wait_ge(osb_done, NO * b + int(what[2]) + 1)
                    transposes(bank, lambda t: osb[:, t * P:(t + 1) * P]).then_inc(OT_filled, 1)
                elif what == "onT":
                    pe.wait_ge(on_done, NO * (b + 1))
                    transposes(bank, lambda t: on[:, t, :]).then_inc(onT_filled, 1)
                elif what == "Wo":
                    pe.wait_ge(onT_done, b + 1)
                    for t in range(NT):
                        last = pe.matmul(bank[:, t * D:(t + 1) * D], onT[:, t * P:(t + 1) * P], wo[:, :],
                                         start=True, stop=True)
                    last.then_inc(Wo_filled, 1)
                elif what == "x2T":
                    pe.wait_ge(x2n_done, NT * (b + 1))
                    transposes(bank, lambda t: x2n[:, t, :]).then_inc(x2T_filled, 1)
                elif what[0] in "gu":
                    j = int(what[1])
                    pe.wait_ge(x2T_done, b + 1)
                    pe.matmul(bank, (wgT if what[0] == "g" else wuT)[:, j, :], x2T[:, :], start=True, stop=True)\
                      .then_inc(g_filled if what[0] == "g" else u_filled, 1)
                else:
                    pe.wait_ge(h_done, NF * (b + 1))
                    half = int(what[1])
                    for t in (2 * half, 2 * half + 1):
                        for j in range(NF):
                            last = pe.matmul(bank[:, t * D:(t + 1) * D], hT[:, j, t * P:(t + 1) * P], wdT[:, j, :],
                                             start=(j == 0), stop=(j == NF - 1))
                    if half == 1:
                        last.then_inc(d_filled, 1)

            def scores_of(i, u, c):
                g, kt = u // NT, u % NT
                at_least(pe, exp_done, 2 * NU * i + 2 * u + c - 1)
                pair = 2 * g + c
                for parity in range(2):
                    last = pe.matmul(scores[:, 2 * c + parity, :], kst[:, pair, kt * P:(kt + 1) * P],
                                     qst[:, pair, parity, :], start=True, stop=True)
                last.then_inc(qk_done, 1)

            def times_v(i, n):
                g, kt = (n % NU) // NT, n % NT
                at_least(pe, exp_done, 2 * NU * i + 2 * n + 2)
                if n % NU in (0, NU // 2):
                    pe.wait_ge(vaugA_done if n % NU == 0 else vaugB_done, i + 1)
                first, last_of_half = n % (NU // NO) == 0, n % (NU // NO) == NU // NO - 1
                if first:
                    at_least(pe, osb_done, NO * i + g // 2)
                for j in range(NG):
                    last = pe.matmul(oacc[STRIP * j:STRIP * (j + 1), :], vaug[:, kt, NG * g + j, :],
                                     probs[:, kt, j, :], start=first, stop=last_of_half)
                last.then_inc(pv_done, 1)

            def row_max_scores(i):
                for h in range(NH):
                    parity, pair = h % 2, h // 2
                    r = slice(HALF * parity, HALF * parity + PART_ROWS)
                    for t in range(NT):
                        n = NT * h + t
                        at_least(pe, mx_taken, NH * NT * i + n - 3 if n >= 4 else NH * NT * i)
                        pe.matmul(scores[:, n % 4, :], qst[r, pair, parity, t * P:(t + 1) * P], kst[r, pair, :],
                                  start=True, stop=True).then_inc(mx_filled, 1)
                wait_apart(pe, mx_taken, NH * NT * (i + 1), passed)
                pe.transpose(scores[0:NH * NT, 0, 0:P], mx[:, :, :], ident[:, :]).then_inc(mxT_filled, 1)
                pe.wait_ge(shift_loaded, 32 * (i + 1))

            for name in PHASE_PIECES["before"]:
                if name == "a_v":
                    pe.wait_ge(w_centred, 1)
                if name == "a_rq":
                    prepare_later_weights()
                piece(name, "before", -1)
            for name in EARLY:
                piece(name, "first", 0)
            pe.wait_ge(wT_copied, 3)
            pe.wait_ge(bo2_done, 1)
            pe.wait_ge(flag_ready, 1)
            needs_max = pe.value_load(flag[0:1, 0:1], min_val=0, max_val=1)

            def turn(i, phase):
                pe.wait_ge(stackA_loaded, 16 * STACK_DMAS * (i + 1))
                with pe.If(needs_max > 0):
                    pe.wait_ge(stackB_loaded, 16 * STACK_DMAS * (i + 1))
                    at_least(pe, exp_done, 2 * NU * i)
                    row_max_scores(i)
                for u in range(NU):
                    if u == NU // 2:
                        pe.wait_ge(stackB_loaded, 16 * STACK_DMAS * (i + 1))
                    slots = {**SIDE, **LAST_SLOTS} if phase == "last" else SIDE
                    here = PHASE_PIECES[phase] + ([] if phase == "first" else ["b_d1"])
                    todo = [p for p in slots.get(u, []) if p in here and not (phase == "first" and p in EARLY)]
                    scores_of(i, u, 0)
                    if u >= 2 or phase != "first":
                        times_v(i, u - 2)
                    scores_of(i, u, 1)
                    for name in todo:
                        piece(name, phase, i)

            turn(0, "first")
            turn(1, "loop")
            with pe.Fori(2, B - 1) as i:
                turn(i, "loop")
            turn(B - 1, "last")
            times_v(B, -2)
            times_v(B, -1)
            pe.wait_ge(y_done, B - 1)
            for half, tiles in enumerate(half_tiles):
                pe.wait_ge(osb_done, NO * (B - 1) + 2 + half)
                transposes(OTs[half], lambda t: osb[:, t * P:(t + 1) * P], tiles).then_inc(OT_filled, 1)
            for half, tiles in enumerate(half_tiles):
                pe.wait_ge(on_done, NO * (B - 1) + 2 + half)
                transposes(onTs[half], lambda t: on[:, t, :], tiles).then_inc(onT_filled, 1)
            for half, tiles in enumerate(half_tiles):
                pe.wait_ge(onT_done, B + half)
                for k, t in enumerate(tiles):
                    last = pe.matmul(Wos[half][:, k * D:(k + 1) * D], onT[:, t * P:(t + 1) * P], wo[:, :],
                                     start=True, stop=True)
                last.then_inc(Wo_filled, 1)

            def last_x2T(half):
                tiles = half_tiles[half]
                pe.wait_ge(x2n_done, NT * (B - 1) + tiles[-1] + 1)
                transposes(x2Ts[half], lambda t: x2n[:, t, :], tiles).then_inc(x2T_filled, 1)

            def last_products(half, banks, w, done):
                cols = half_cols[half]
                for j in range(NF):
                    last = pe.matmul(banks[j][:, cols], w[:, j, :], x2T[:, cols], start=True, stop=True)
                    if half == 1:
                        last.then_inc(done, 1)

            last_x2T(0)
            pe.wait_ge(x2T_done, B)
            last_products(0, last_gates, wgT, g_filled)
            last_x2T(1)
            last_products(0, last_ups, wuT, u_filled)
            pe.wait_ge(x2T_done, B + 1)
            last_products(1, last_gates, wgT, g_filled)
            last_products(1, last_ups, wuT, u_filled)
            for j in range(NF):
                pe.wait_ge(h_done, NF * (B - 1) + j + 1)
                for t in range(NT):
                    down = pe.matmul(last_downs[t], hT[:, j, t * P:(t + 1) * P], wdT[:, j, :],
                                     start=(j == 0), stop=(j == NF - 1))
                    if j == NF - 1:
                        down.then_inc(d_filled, 1)

        @block.vector
        def _(dve):
            def centre_weights():
                dve.wait_ge(w_loaded, 16 * N_W)
                heads = wraw[:, :, :].rearrange("p k (h d) -> p (k h) d", d=HD)
                dve.reduce_sum(head_sum[:, :], heads, AX.X).then_inc(head_sums_done, 1)
                dve.wait_ge(head_sums_done, 1)
                dve.scalar_tensor_tensor(out=wqkv[:, :, :].rearrange("p k (h d) -> p (k h) d", d=HD),
                                         in0=head_sum[:, :].unsqueeze(2).broadcast_to((P, 4 * NH, HD)),
                                         scalar=-1.0 / HD, in1=heads, op0=ALU.mult, op1=ALU.add).then_inc(w_centred, 1)

            def centre_biases():
                dve.wait_ge(bias_filled, 1)
                dve.tensor_copy(bias_cen[:, :], scores[:, 0, 0:2]).then_inc(bias_centred, 1)

            def prepare_small():
                dve.wait_ge(aux_loaded, 16 * N_AUX)
                dve.tensor_scalar(q_aff[:, :], affine[:, 0:2], HD ** -0.5, None, ALU.mult).then_inc(small_done, 1)
                dve.tensor_copy(vb_rep[:, :], affine[:, 5:6].broadcast_to((P, P))).then_inc(small_done, 1)
                dve.tensor_scalar(wo[:, :], wo_raw[:, :], affine[:, 4:5], None, ALU.mult).then_inc(small_done, 1)

            def output_bias():
                dve.wait_ge(bo2_filled, 1)
                dve.tensor_tensor(out=bo2_row[:, :], in0=scores[:, 3, 0:D], in1=bo_row[:, :], op=ALU.add)\
                   .then_inc(bo2_done, 1)

            def score_bound():
                steps = [0]

                def link(ins):
                    steps[0] += 1
                    ins.then_inc(bound_step, 1)
                    dve.wait_ge(bound_step, steps[0])
                dve.wait_ge(prm_loaded, 64)
                link(dve.tensor_tensor(out=prm2[:, :, :], in0=prm[:, :, :], in1=prm[:, :, :], op=ALU.mult))
                link(dve.reduce_max(bnd[:, 0:2], prm2[:, 0:4:2, :], AX.X))
                link(dve.reduce_sum(bnd[:, 2:4], prm2[:, 1:4:2, :], AX.X))
                link(dve.scalar_tensor_tensor(out=bnd[:, 4:6], in0=bnd[:, 0:2], scalar=float(HD), in1=bnd[:, 2:4],
                                              op0=ALU.mult, op1=ALU.add))
                link(dve.tensor_tensor(out=bnd[:, 6:7], in0=bnd[:, 4:5], in1=bnd[:, 5:6], op=ALU.mult))
                link(dve.tensor_scalar(bnd[:, 7:8], bnd[:, 6:7], SCORE_BOUND ** 2 * HD / 4, -1.0, ALU.is_le, ALU.mult))
                dve.tensor_scalar(flag[:, :], bnd[:, 7:8], 1.0, None, ALU.add).then_inc(flag_ready, 1)

            def norm_stats(b, src, stats, mv, src_ready, stats_done, mv_done, tiles=range(NT)):
                src_ready()
                for t in tiles:
                    dve.bn_stats(stats[:, t, :], src[:, t, :]).then_inc(stats_done, 1)
                for t in tiles:
                    wait_apart(dve, stats_done, NT * b + t + 1, passed)
                    dve.bn_aggr(mv[:, t, :], stats[:, t, :]).then_inc(mv_done, 1)

            def norm_apply(b, src, dst, mv, rs, rs_done, done, half=None):
                tiles, n = (range(NT), 0) if half is None else (half_tiles[half], half)
                dve.wait_ge(rs_done, b + 1 + n)
                for t in tiles:
                    dve.tensor_scalar(dst[:, t, :], src[:, t, :], mv[:, t, 0:1], rs[:, t:t + 1],
                                      ALU.subtract, ALU.mult).then_inc(done, 1)

            def ln1_stats(b):
                norm_stats(b, x_in, stats1, mv1, lambda: dve.wait_ge(x_loaded, 16 * (b + 1)), stats1_done, mv1_done)

            def ln1_apply(b):
                norm_apply(b, x_in, xn, mv1, rs1, rs1_done, xn_done)

            def copy_xT(b):
                dve.wait_ge(xT_filled, b + 1)
                dve.tensor_copy(xnT[:, :], side[:, BANK["a_xT"], :])\
                   .then_inc(xnT_done, 1)

            def centred(b, w):
                name, sem_f = (("a_q", q_filled), ("a_k", k_filled))[w]
                dve.wait_ge(sem_f, b + 1)
                dve.tensor_scalar(qk_c[:, w, :], side[:, BANK[name], :], bias_cen[:, w:w + 1], None, ALU.add)\
                   .then_inc(qkc_done, 1)

            def centred_v(b):
                dve.wait_ge(v_filled, b + 1)
                at_least(dve, vaugB_done, b)
                dve.tensor_tensor(out=v_c[:, :, :],
                                  in0=side[:, BANK["a_v"], :].rearrange("p (t d) -> p t d", t=NT),
                                  in1=wqkv[:, 3, :].unsqueeze(1).broadcast_to((P, NT, D)), op=ALU.add)\
                   .then_inc(vc_done, 1)

            def variances(b):
                dve.wait_ge(vsq_done, b + 1)
                dve.reduce_sum(v_sum[:, :], v_sq[:, :, :].rearrange("p t (h d) -> p (t h) d", d=HD), AX.X)\
                   .then_inc(vsum_done, 1)
                dve.wait_ge(var_filled, b + 1)
                dve.tensor_scalar(hv[:, 0:2, :, :].rearrange("p w t h -> p (w t h)"),
                                  side[:, BANK["a_var"], 0:2 * NT * NH], HEAD_EPS, None, ALU.add)\
                   .then_inc(hv_done, 1)
                dve.wait_ge(vsum_done, b + 1)
                dve.tensor_scalar(hv[:, 2, :, :].rearrange("p t h -> p (t h)"), v_sum[:, :], 1.0 / HD, HEAD_EPS,
                                  ALU.mult, ALU.add).then_inc(hv_done, 1)
                dve.wait_ge(hv_done, 2 * (b + 1))
                dve.tensor_scalar(hy[:, :, :, :].bitcast(I32), hv[:, :, :, :].bitcast(I32), -0.5, RSQRT_SEED,
                                  ALU.mult, ALU.add).then_inc(seed_done, 1)
                dve.wait_ge(seed_done, b + 1)
                newton_step(b, 0)

            v_all, y_all, t_all = (z[:, :, :, :].rearrange("p w t h -> p (w t h)") for z in (hv, hy, ht))

            def newton_step(b, k):
                def step(ins, n):
                    ins.then_inc(newton, 1)
                    dve.wait_ge(newton, 8 * b + 3 * k + n)
                step(dve.tensor_tensor(out=t_all, in0=y_all, in1=y_all, op=ALU.mult), 1)
                step(dve.scalar_tensor_tensor(out=t_all, in0=t_all, scalar=-0.5, in1=v_all,
                                              op0=ALU.mult, op1=ALU.mult), 2)
                if k < 2:
                    step(dve.scalar_tensor_tensor(out=y_all, in0=t_all, scalar=1.5, in1=y_all,
                                                  op0=ALU.add, op1=ALU.mult), 3)

            def rsqrt_end(b):
                newton_step(b, 1)
                newton_step(b, 2)
                n = NT * NH
                for w in range(2):
                    dve.scalar_tensor_tensor(out=hyx[:, w, :, :, :].rearrange("p t h d -> p (t h) d"),
                                             in0=t_all[:, w * n:(w + 1) * n].unsqueeze(2).broadcast_to((P, n, HD)),
                                             scalar=1.5,
                                             in1=y_all[:, w * n:(w + 1) * n].unsqueeze(2).broadcast_to((P, n, HD)),
                                             op0=ALU.add, op1=ALU.mult).then_inc(rsqrt_done, 1)
                dve.scalar_tensor_tensor(out=y_all[:, 2 * n:], in0=t_all[:, 2 * n:], scalar=1.5, in1=y_all[:, 2 * n:],
                                         op0=ALU.add, op1=ALU.mult).then_inc(rsqrt_done, 1)

            def normed(b):
                for w, name in enumerate(("a_rq", "a_rk")):
                    dve.wait_ge(r_filled, 2 * b + w + 1)
                    dve.tensor_tensor(out=qk_n[:, w, :], in0=side[:, BANK[name], :], in1=qk_c[:, w, :], op=ALU.mult)\
                       .then_inc(qkn_done, 1)
                for w in range(2):
                    sc, bi = ((q_aff[:, 0:1], q_aff[:, 1:2]), (affine[:, 2:3], affine[:, 3:4]))[w]
                    dve.wait_ge(qkn_done, 2 * b + w + 1)
                    dve.tensor_scalar(qk_f[:, w, :], qk_n[:, w, :], sc, bi, ALU.mult, ALU.add).then_inc(qkf_done, 1)
                at_least(dve, parts_stored, 16 * PART_DMAS * b)
                dve.wait_ge(qkf_done, 2 * (b + 1))
                dve.tensor_copy(parts[:, 0, :, :], qk_f[:, :, :]).then_inc(part_done, 1)
                dve.wait_ge(part_done, 3 * b + 1)
                dve.tensor_tensor(out=qk_r[:, :, :], in0=qk_f[:, :, :], in1=parts[:, 0, :, :], op=ALU.subtract)\
                   .then_inc(rest_done, 1)

            def lower_parts(b):
                dve.wait_ge(rest_done, b + 1)
                dve.tensor_copy(parts[:, 1, :, :], qk_r[:, :, :]).then_inc(part_done, 1)
                dve.wait_ge(part_done, 3 * b + 2)
                dve.tensor_tensor(out=parts[:, 2, :, :], in0=qk_r[:, :, :], in1=parts[:, 1, :, :], op=ALU.subtract)\
                   .then_inc(part_done, 1)

            def fill_v(b, half):
                at_least(dve, pv_done, NU * b - (NU // 2 if half == 0 else 0))
                if half == 0:
                    dve.wait_ge(rsqrt_done, 3 * (b + 1))
                for k in range(2):
                    hs = slice(NG * (2 * half + k), NG * (2 * half + k + 1))
                    v = v_c[:, :, :].rearrange("p t (h d) -> p t h d", d=HD)[:, :, hs, :]
                    last = dve.tensor_tensor(out=vaug[:, :, hs, HC * k:HC * k + HD], in0=v,
                                             in1=hy[:, 2, :, hs].unsqueeze(3).broadcast_to((P, NT, NG, HD)),
                                             op=ALU.mult)
                last.then_inc(vaugA_done if half == 0 else vaugB_done, 1)

            def divide(b, half):
                o = side[:, BANK[("c_OT0", "b_OT1")[half]], :].rearrange("p (t j x) -> p t j x", t=NT, j=NG)
                dve.wait_ge(OT_filled, NO * b + half + 1)
                if half == 0:
                    at_least(dve, onT_filled, b)
                at_least(dve, on_done, NO * b + half)
                for k in range(2):
                    last = dve.reciprocal(rinv[:, k, :, :], o[:, :, :, HC * k + HD])
                last.then_inc(rinv_done, 1)
                dve.wait_ge(rinv_done, NO * b + half + 1)
                for k in range(2):
                    h0 = NG * (2 * half + k)
                    last = dve.tensor_tensor(
                        out=on[:, :, h0 * HD:(h0 + NG) * HD].rearrange("p t (j d) -> p t j d", d=HD),
                        in0=o[:, :, :, HC * k:HC * k + HD],
                        in1=rinv[:, k, :, :].unsqueeze(3).broadcast_to((P, NT, NG, HD)), op=ALU.mult)
                last.then_inc(on_done, 1)

            def copy_onT(b):
                dve.wait_ge(onT_filled, b + 1)
                dve.tensor_copy(onT[:, :], side[:, BANK["b_onT"], :])\
                   .then_inc(onT_done, 1)

            def ln2_stats(b):
                dve.wait_ge(Wo_filled, b + 1)
                dve.wait_ge(xbo_done, b + 1)
                dve.tensor_tensor(out=x2[:, :, :], in0=side[:, BANK["b_Wo"], :].rearrange("p (t d) -> p t d", t=NT),
                                  in1=x_bo[:, :, :], op=ALU.add).then_inc(x2_done, 1)
                norm_stats(b, x2, stats2, mv2, lambda: dve.wait_ge(x2_done, b + 1), stats2_done, mv2_done)

            def ln2_apply(b):
                norm_apply(b, x2, x2n, mv2, rs2, rs2_done, x2n_done)

            def copy_x2T(b):
                dve.wait_ge(x2T_filled, b + 1)
                dve.tensor_copy(x2T[:, :], side[:, BANK["b_x2T"], :])\
                   .then_inc(x2T_done, 1)

            def silu(b, j, gate):
                dve.wait_ge(tanh_done, NF * b + j + 1)
                dve.scalar_tensor_tensor(out=ga[:, j, :], in0=th[:, j, :], scalar=1.0, in1=gate,
                                         op0=ALU.add, op1=ALU.mult)\
                   .then_inc(ga_done, 1)

            def times_up(b, j, up):
                dve.wait_ge(u_filled, NF * b + j + 1)
                dve.wait_ge(ga_done, NF * b + j + 1)
                dve.tensor_tensor(out=hT[:, j, :], in0=up, in1=ga[:, j, :], op=ALU.mult)\
                   .then_inc(h_done, 1)

            def silu_up(b, j):
                silu(b, j, side[:, BANK[f"b_g{j}"], :])
                times_up(b, j, side[:, BANK[f"b_u{j}"], :])

            def result(b):
                dve.wait_ge(d_filled, b + 1)
                at_least(dve, out_stored, 16 * b)
                dve.tensor_tensor(out=y[:, :, :], in0=side[:, BANK["b_d0"], :].rearrange("p (t d) -> p t d", t=NT),
                                  in1=x2[:, :, :], op=ALU.add).then_inc(y_done, 1)

            def row_maxima(i):
                for n in range(NH * NT):
                    dve.wait_ge(mx_filled, NH * NT * i + n + 1)
                    dve.tensor_reduce(out=mx[:, n // NT, n % NT:n % NT + 1], in_=scores[:, n % 4, :], axis=AX.X,
                                      op=ALU.max, negate=True).then_inc(mx_taken, 1)
                dve.wait_ge(mxT_filled, i + 1)
                at_least(dve, maxes_stored, 32 * i)
                dve.tensor_copy(mx_hi[:, :], scores[0:NH * NT, 0, 0:P]).then_inc(mx_parts, 1)
                dve.wait_ge(mx_parts, 2 * i + 1)
                dve.tensor_tensor(out=mx_lo[:, :], in0=scores[0:NH * NT, 0, 0:P], in1=mx_hi[:, :], op=ALU.subtract)\
                   .then_inc(mx_parts, 1)

            ln1_stats(0)
            ln1_apply(0)
            centre_weights()
            copy_xT(0)
            centre_biases()
            ln1_stats(1)
            centred_v(0)
            dve.wait_ge(bias_centred, 1)
            centred(0, 0)
            centred(0, 1)
            score_bound()
            variances(0)
            prepare_small()
            rsqrt_end(0)
            ln1_apply(1)
            dve.wait_ge(small_done, 3)
            normed(0)
            lower_parts(0)
            output_bias()
            dve.wait_ge(consts, 3)
            fill_v(0, 0)
            centred(1, 0)
            centred(1, 1)
            fill_v(0, 1)
            centred_v(1)
            variances(1)
            dve.wait_ge(flag_ready, 1)
            needs_max = dve.value_load(flag[0:1, 0:1], min_val=0, max_val=1)

            def turn(i, phase):
                ahead = phase in ("first", "loop")
                behind = phase != "first"
                with dve.If(needs_max > 0):
                    row_maxima(i)
                if phase == "loop":
                    ln1_stats(i + 1)
                    ln1_apply(i + 1)
                    copy_xT(i + 1)
                if phase != "first":
                    fill_v(i, 1)
                if behind:
                    divide(i - 1, 1)
                if phase == "loop":
                    centred(i + 1, 0)
                if behind:
                    copy_onT(i - 1)
                if phase == "loop":
                    centred(i + 1, 1)
                if behind:
                    ln2_stats(i - 1)
                if phase == "loop":
                    centred_v(i + 1)
                if behind:
                    ln2_apply(i - 1)
                if phase == "loop":
                    variances(i + 1)
                if behind:
                    copy_x2T(i - 1)
                if ahead:
                    rsqrt_end(i + 1)
                    normed(i + 1)
                if behind:
                    silu_up(i - 1, 0)
                if ahead:
                    lower_parts(i + 1)
                if behind:
                    silu_up(i - 1, 1)
                divide(i, 0)
                if ahead:
                    fill_v(i + 1, 0)
                if behind:
                    silu_up(i - 1, 2)
                    result(i - 1)

            turn(0, "first")
            turn(1, "loop")
            with dve.Fori(2, B - 1) as i:
                turn(i, "loop")
            turn(B - 1, "last")
            lastO = NO * (B - 1)
            dve.wait_ge(on_done, lastO + 1)
            for half in range(2):
                ts = slice(half * HALF_TILES, (half + 1) * HALF_TILES)
                o = OTs[half][:, 0:S // 2].rearrange("p (t j x) -> p t j x", t=HALF_TILES, j=NG)
                dve.wait_ge(OT_filled, lastO + 2 + half)
                for k in range(2):
                    last = dve.reciprocal(rinv[:, k, ts, :], o[:, :, :, HC * k + HD])
                last.then_inc(rinv_done, 1)
                dve.wait_ge(rinv_done, lastO + 2 + half)
                for k in range(2):
                    h0 = NG * (2 + k)
                    last = dve.tensor_tensor(
                        out=on[:, ts, h0 * HD:(h0 + NG) * HD].rearrange("p t (j d) -> p t j d", d=HD),
                        in0=o[:, :, :, HC * k:HC * k + HD],
                        in1=rinv[:, k, ts, :].unsqueeze(3).broadcast_to((P, HALF_TILES, NG, HD)), op=ALU.mult)
                last.then_inc(on_done, 1)
            for half, cols in enumerate(half_cols):
                dve.wait_ge(onT_filled, B + half)
                dve.tensor_copy(onT[:, cols], onTs[half][:, 0:S // 2]).then_inc(onT_done, 1)
            dve.wait_ge(xbo_done, B)
            for half in range(2):
                ts = slice(half * HALF_TILES, (half + 1) * HALF_TILES)
                dve.wait_ge(Wo_filled, B + half)
                dve.tensor_tensor(out=x2[:, ts, :],
                                  in0=Wos[half][:, 0:S // 2].rearrange("p (t d) -> p t d", t=HALF_TILES),
                                  in1=x_bo[:, ts, :], op=ALU.add).then_inc(x2_done, 1)
                norm_stats(B - 1, x2, stats2, mv2, lambda: dve.wait_ge(x2_done, B + half), stats2_done, mv2_done,
                           half_tiles[half])
            for half in range(2):
                norm_apply(B - 1, x2, x2n, mv2, rs2, rs2_done, x2n_done, half)
            for half, cols in enumerate(half_cols):
                dve.wait_ge(x2T_filled, B + half)
                dve.tensor_copy(x2T[:, cols], x2Ts[half][:, 0:S // 2]).then_inc(x2T_done, 1)
            silu(B - 1, 0, last_gates[0])
            for j in range(NF):
                if j + 1 < NF:
                    silu(B - 1, j + 1, last_gates[j + 1])
                times_up(B - 1, j, last_ups[j])
            dve.wait_ge(out_stored, 16 * (B - 1))
            for t in range(NT):
                dve.wait_ge(d_filled, B + t)
                last = dve.tensor_tensor(out=y[:, t, :], in0=last_downs[t], in1=x2[:, t, :], op=ALU.add)
            last.then_inc(y_done, 1)


INPUTS = ["L0_attn_x", "L0_attn_Wq", "L0_attn_bq", "L0_attn_Wk", "L0_attn_bk", "L0_attn_Wv", "L0_attn_bv",
          "L0_attn_q_scale", "L0_attn_q_bias", "L0_attn_k_scale", "L0_attn_k_bias", "L0_attn_v_scale",
          "L0_attn_v_bias", "L0_attn_Wo", "L0_attn_bo", "L0_ffn_w_gate", "L0_ffn_w_up", "L0_ffn_w_down"]


def kernel(**inputs):
    from concourse import bacc
    from concourse.bass_utils import run_bass_kernel_spmd

    nc = bacc.Bacc("TRN2", target_bir_lowering=False, num_devices=1)
    arrays, args = {}, []
    for name in INPUTS:
        a = np.ascontiguousarray(inputs[name])
        arrays["in_" + name] = a
        args.append(nc.dram_tensor("in_" + name, a.shape, mybir.dt.from_np(a.dtype), kind="ExternalInput").ap())
    parts = nc.dram_tensor("parts_dram", (2, P, 6, S), BF16, kind="Internal").ap()
    maxes = nc.dram_tensor("maxes_dram", (2, NH, NT, P), BF16, kind="Internal").ap()
    out = nc.dram_tensor("out_dram", (B, S, D), F32, kind="ExternalOutput").ap()
    build(nc, *args, parts, maxes, out)
    r = run_bass_kernel_spmd(nc, [arrays], core_ids=[0])
    return r.results[0]["out_dram"]
```
